# Optimizing a Trainium2 kernel written in Bass

```python
import numpy as np
import jax
import jax.numpy as jnp

def _softmax(x, axis=-1):
    return jax.nn.softmax(x, axis=axis)

def _gelu(x):
    return jax.nn.gelu(x, approximate=True)

def _silu(x):
    return jax.nn.silu(x)

def _sigmoid(x):
    return jax.nn.sigmoid(x)

def _layernorm(x, axis=-1, eps=1e-05):
    m = jnp.mean(x, axis=axis, keepdims=True)
    v = jnp.var(x, axis=axis, keepdims=True)
    return (x - m) / jnp.sqrt(v + eps)

def _scatter_add(tgt, idx, src, axis=0):
    return tgt.at[idx].add(src)

def _segment_sum(src, seg, n):
    return jax.ops.segment_sum(src, seg, n)
kernel_name = 'mk_pixart_resid_d1_seqx_r8_e7ac68'

def setup_inputs(seed: int=0):
    np.random.seed(seed)
    _w = jnp.asarray

    def _rec_inputs():
        import jax
        import jax.numpy as jnp
        _rk = jax.random.key(seed)
        x = 2.818e-05 + 1 * jax.random.normal(jax.random.fold_in(_rk, 1), (32, 128, 128), jnp.float32)
        _lenS = 128 - jax.random.randint(jax.random.fold_in(_rk, 7), (32,), 0, max(1, 128 // 4) + 1, jnp.int32)
        _lenS2 = 128 - jax.random.randint(jax.random.fold_in(_rk, 8), (32,), 0, max(1, 128 // 4) + 1, jnp.int32)
        _ctx_1024P = jax.random.normal(jax.random.fold_in(_rk, 11), (32, 16, 128), jnp.float32)
        _ctx_1024c = jax.random.dirichlet(jax.random.fold_in(_rk, 511), 0.3 * jnp.ones((16,), jnp.float32), (32, 128))
        _ctx_1024t = jnp.einsum('bsk,bkd->bsd', _ctx_1024c, _ctx_1024P)
        _ctx_1024t = _ctx_1024t * jax.lax.rsqrt(jnp.mean(jnp.square(_ctx_1024t)) + 1e-12) * 0.953939
        ctx_1024 = -0.000391444 + 0.999954 * (_ctx_1024t + 0.3 * jax.random.normal(jax.random.fold_in(_rk, 611), (32, 128, 128), jnp.float32))
        condB_pt = jax.random.uniform(jax.random.fold_in(_rk, 13), (32,), jnp.float32, 0.0, 226.919)
        return (x, ctx_1024, condB_pt, _lenS2)
    x, ctx_1024, condB_pt, _lenS2 = _rec_inputs()

    def _L0_xcond_setup():
        import jax, jax.numpy as jnp
        import numpy as np
        N, L, H, Q = (64, 258, 128, 32)
        WINDOW = 16.0
        DEV_POW = 128.0
        key = jax.random.key(seed)
        k1, k2, k3, k4, k5, k6 = jax.random.split(key, 6)
        encoder_outputs = jax.random.normal(k1, (N, L, H), dtype=jnp.float32)
        decoder_h_t = jax.random.normal(k2, (N, Q, H), dtype=jnp.float32)
        src_len = jax.random.randint(k3, (N,), 32, L + 1).astype(jnp.int32)
        p_t = jax.random.uniform(k4, (N,), dtype=jnp.float32) * (src_len.astype(jnp.float32) - 1.0)
        W_a = jax.random.normal(k5, (H, H), dtype=jnp.float32) * (1.0 / np.sqrt(H))
        W_c = jax.random.normal(k6, (H, 2 * H), dtype=jnp.float32) * (1.0 / np.sqrt(2 * H))
        return {'encoder_outputs': encoder_outputs, 'decoder_h_t': decoder_h_t, 'src_len': src_len, 'p_t': p_t, 'W_a': W_a, 'W_c': W_c}
    _L0_xcond_all = _L0_xcond_setup()
    _L0_xcond_in = {k: v for k, v in _L0_xcond_all.items() if k in ('W_a', 'W_c')}
    del _L0_xcond_all

    def _L0_ffn_setup():
        import jax, jax.numpy as jnp
        import numpy as np
        B, P, D, D_MLP, E, K = (2, 256, 128, 512, 8, 2)
        key = jax.random.key(seed)
        k_x, k_g, k_in, k_out = jax.random.split(key, 4)
        s_in = 1.0 / np.sqrt(D).astype(np.float32)
        s_out = 1.0 / np.sqrt(D_MLP).astype(np.float32)
        return {'x': jax.random.normal(k_x, (B, P, D), dtype=jnp.float32), 'W_gate': jax.random.normal(k_g, (D, E), dtype=jnp.float32) * s_in, 'W_in': jax.random.normal(k_in, (E, D, D_MLP), dtype=jnp.float32) * s_in, 'b_in': jnp.zeros((E, D_MLP), dtype=jnp.float32), 'W_out': jax.random.normal(k_out, (E, D_MLP, D), dtype=jnp.float32) * s_out, 'b_out': jnp.zeros((E, D), dtype=jnp.float32)}
    _L0_ffn_all = _L0_ffn_setup()
    _L0_ffn_in = {k: v for k, v in _L0_ffn_all.items() if k in ('W_gate', 'W_in', 'b_in', 'W_out', 'b_out')}
    del _L0_ffn_all
    return {'x': x, 'ctx_1024': ctx_1024, 'condB_pt': condB_pt, '_lenS2': _lenS2, 'L0_xcond_W_a': _L0_xcond_in['W_a'], 'L0_xcond_W_c': _L0_xcond_in['W_c'], 'L0_ffn_W_gate': _L0_ffn_in['W_gate'], 'L0_ffn_W_in': _L0_ffn_in['W_in'], 'L0_ffn_b_in': _L0_ffn_in['b_in'], 'L0_ffn_W_out': _L0_ffn_in['W_out'], 'L0_ffn_b_out': _L0_ffn_in['b_out']}

def reference(x, ctx_1024, condB_pt, _lenS2, L0_xcond_W_a, L0_xcond_W_c, L0_ffn_W_gate, L0_ffn_W_in, L0_ffn_b_in, L0_ffn_W_out, L0_ffn_b_out):
    import jax
    import jax.numpy as jnp

    def _L0_xcond_ref(encoder_outputs, decoder_h_t, src_len, p_t, W_a, W_c):
        import jax, jax.numpy as jnp
        import numpy as np
        N, L, H, Q = (64, 258, 128, 32)
        WINDOW = 16.0
        DEV_POW = 128.0
        n, l, h = encoder_outputs.shape
        idx = jnp.arange(l, dtype=jnp.float32)
        src_end = src_len.astype(jnp.float32)
        attn_start = jnp.maximum(p_t - WINDOW, 0.0)
        attn_end = jnp.minimum(p_t + WINDOW, src_end)
        mask = (idx[None, :] < attn_start[:, None]) | (idx[None, :] > attn_end[:, None])
        score = jnp.einsum('nqh,hk,nlk->nql', decoder_h_t, W_a, encoder_outputs)
        score = jnp.where(mask[:, None, :], -1000000000.0, score)
        align = jax.nn.softmax(score, axis=2)
        gauss = jnp.exp(-(idx[None, :] - p_t[:, None]) ** 2 / DEV_POW)
        align = align * gauss[:, None, :]
        context = jnp.einsum('nql,nlh->nqh', align, encoder_outputs)
        cat = jnp.concatenate([context, decoder_h_t], axis=2)
        return jnp.tanh(cat @ W_c.T)

    def _L0_ffn_ref(x, W_gate, W_in, b_in, W_out, b_out):
        import jax, jax.numpy as jnp
        import numpy as np
        B, P, D, D_MLP, E, K = (2, 256, 128, 512, 8, 2)
        gate_logits = jnp.einsum('bpd,de->bpe', x, W_gate)
        top_w, top_idx = jax.lax.top_k(gate_logits, K)
        top_w = jax.nn.softmax(top_w, axis=-1)
        combine = jnp.einsum('bpke,bpk->bpe', jax.nn.one_hot(top_idx, E, dtype=x.dtype), top_w)
        out = jnp.zeros_like(x)
        for e in range(E):
            h = jax.nn.gelu(jnp.einsum('bpd,dm->bpm', x, W_in[e]) + b_in[e], approximate=False)
            y = jnp.einsum('bpm,md->bpd', h, W_out[e]) + b_out[e]
            out = out + combine[..., e, None] * y
        return out
    x = x + _L0_xcond_ref(ctx_1024, _layernorm(x, axis=-1), _lenS2, condB_pt, L0_xcond_W_a, L0_xcond_W_c)
    x = x + _L0_ffn_ref(_layernorm(x, axis=-1), L0_ffn_W_gate, L0_ffn_W_in, L0_ffn_b_in, L0_ffn_W_out, L0_ffn_b_out)
    return x

_drawn_inputs = setup_inputs


def setup_inputs(seed=0):
    import zlib

    import numpy as np

    out = dict(_drawn_inputs(seed))
    spreads = {'L0_ffn_b_in': (0.0, 0.1), 'L0_ffn_b_out': (0.0, 0.1)}
    factors = {}
    for name, (base, spread) in spreads.items():
        noise = np.random.default_rng([zlib.crc32(name.encode()), seed]).standard_normal(out[name].shape)
        drawn = base * np.exp(spread * noise) if base else spread * noise
        out[name] = jnp.asarray(drawn.astype(out[name].dtype))
    for name, factor in factors.items():
        out[name] = (out[name] * factor).astype(out[name].dtype)
    return out
```

```python
import numpy as np
import concourse.bass as bass
from concourse import mybir
from contextlib import ExitStack

F32 = mybir.dt.float32
F32R = mybir.dt.float32r
BF16 = mybir.dt.bfloat16
I32 = mybir.dt.int32
U32 = mybir.dt.uint32
ALU = mybir.AluOpType
ACT = mybir.ActivationFunctionType
AX = mybir.AxisListType.X

P = 128
NB = 32
GB = 4
NG = NB // GB
NH = 2
HB = NB // NH
HG = NG // NH
E = 8
K = 2
M = 512
MC = M // P
ST = (HB * P * K + E * (P - 1)) // P
T = NH * ST
ROW = 132
TOKEN, SECOND = P, P + 1
NROWS = NB * P * K
SKIP = 65536.0
UN = 4
WCH = 1024
EPS = 1e-5
WINDOW = 16.0
DEV_POW = 128.0


def build(nc, x, ctx_in, pt, lens, w_a, w_c, w_gate, w_in, b_in, w_out, b_out, out):
    slots = nc.dram_tensor("slots", [T * P, ROW], F32, kind="Internal").ap()
    eout = nc.dram_tensor("eout", [NROWS, P], F32, kind="Internal").ap()
    win_d = nc.dram_tensor("win_d", [NB, 2 * P], F32, kind="Internal").ap()
    with ExitStack() as es:
        def sb(name, shape, dt=F32):
            return es.enter_context(nc.sbuf_tensor(name, shape, dt))

        def sem(name):
            return es.enter_context(nc.semaphore(name))

        bank = [es.enter_context(nc.psum_tensor(f"bank{i}", [P, 512], F32)) for i in range(8)]
        p_encT = p_G = bank[0]
        p_xnT, p_V, p_log, p_S, p_alT, p_O, p_xmT = bank[1], bank[2], bank[3], bank[4], bank[5], bank[6], bank[7]
        p_rank, p_cnt = bank[3][:, 128:256], bank[3][:, 256:256 + E]
        p_H, p_hT, p_xT, p_Y = [bank[0], bank[1]], [bank[4], bank[5]], bank[7], bank[6]

        ident = sb("ident", [P, P])
        tri = sb("tri", [P, P], BF16)
        ones_b = sb("ones_b", [P, P], BF16)
        neg = sb("neg", [P, 512])
        mhalf, epsc = sb("mhalf", [P, GB]), sb("epsc", [P, GB])
        revidx = sb("revidx", [P, E])
        caps = sb("caps", [P, 16])
        ones8 = sb("ones8", [P, E])
        tilei = sb("tilei", [P, ST])
        filler = sb("filler", [P, ROW])
        wa, wc = sb("wa", [P, P]), sb("wc", [P, 2 * P])
        waT, wcT = sb("waT", [P, P]), sb("wcT", [P, 2, P])
        wg = sb("wg", [P, E])
        wraw = sb("wraw", [P, 2, WCH])
        wi_hi, wi_lo = sb("wi_hi", [P, E * M], F32R), sb("wi_lo", [P, E * M], F32R)
        wo_hi, wo_lo = sb("wo_hi", [P, E * M], F32R), sb("wo_lo", [P, E * M], F32R)
        binb, boutb = sb("binb", [P, E * M]), sb("boutb", [P, E * P])
        ptc, lenc, lenf = sb("ptc", [NB, 1]), sb("lenc", [NB, 1], I32), sb("lenf", [NB, 1])
        idx = sb("idx", [NB, P])
        w_lo, w_hi = sb("w_lo", [NB, 1]), sb("w_hi", [NB, 1])
        below, dist, dist2 = sb("below", [NB, P]), sb("dist", [NB, P]), sb("dist2", [NB, P])
        above = sb("above", [NB, P])
        winall = sb("winall", [NB, 2 * P])
        xs = sb("xs", [P, NB, P])
        enc = sb("enc", [P, 2, GB, P])
        win = sb("win", [P, 2, GB, 2, P])
        st1, mv1 = sb("st1", [P, 2, GB, 6]), sb("mv1", [P, 2, GB, 2])
        ve1, rs1 = sb("ve1", [P, 2, GB]), sb("rs1", [P, 2, GB])
        st2, mv2 = sb("st2", [P, 2, GB, 6]), sb("mv2", [P, 2, GB, 2])
        ve2, rs2 = sb("ve2", [P, 2, GB]), sb("rs2", [P, 2, GB])
        xn, xnT = sb("xn", [P, 2, GB, P]), sb("xnT", [P, 2, GB, P])
        encT, Gs, Vs = sb("encT", [P, GB, P]), sb("Gs", [P, GB, P]), sb("Vs", [P, 2, GB, P])
        nmax, ssum, rinv = sb("nmax", [P, 2, GB]), sb("ssum", [P, 2, GB]), sb("rinv", [P, 2, GB])
        ex, al, alT = sb("ex", [P, GB, P]), sb("al", [P, GB, P]), sb("alT", [P, GB, P])
        xm, xmT = sb("xm", [P, 2, GB, P]), sb("xmT", [P, GB, P])
        rows = sb("rows", [P, NB, ROW])
        logits = sb("logits", [P, NB, E])
        idle_v, idle_p = sb("idle_v", [1, 1]), sb("idle_p", [1, 1])
        r1, r2, r3 = (sb(n, [P, HB, E]) for n in ("r1", "r2", "r3"))
        oh1, oh2 = sb("oh1", [P, HB, E]), sb("oh2", [P, HB, E])
        cnt = sb("cnt", [P, HB, E], BF16)
        m1, m2, k1, k2 = (sb(n, [P, HB]) for n in ("m1", "m2", "k1", "k2"))
        md, me, mw = (sb(n, [P, HB]) for n in ("md", "me", "mw"))
        wt = sb("wt", [P, K, NB])
        nexp, cover = sb("nexp", [P, E]), sb("cover", [P, E, 16])
        tiles_e, cum, base = sb("tiles_e", [P, E]), sb("cum", [P, E]), sb("base", [P, E])
        pos = sb("pos", [P, HB, E])
        slotf, slot = sb("slotf", [P, K, HB]), sb("slot", [P, K, NB], U32)
        ecmp, eraw = sb("ecmp", [P, ST, E]), sb("eraw", [P, ST])
        eidf, eidi = sb("eidf", [P, T]), sb("eidi", [P, T], I32)
        xin = [sb(f"xin{i}", [P, ROW]) for i in range(UN)]
        xhi = [sb(f"xhi{i}", [P, P], F32R) for i in range(2)]
        xlo = [sb(f"xlo{i}", [P, P], F32R) for i in range(2)]
        pre = [sb(f"pre{i}", [P, M]) for i in range(2)]
        hid = [sb(f"hid{i}", [P, M]) for i in range(2)]
        hhi = [sb(f"hhi{i}", [P, M], F32R) for i in range(2)]
        hlo = [sb(f"hlo{i}", [P, M], F32R) for i in range(2)]
        ys = [sb(f"ys{i}", [P, P]) for i in range(UN)]
        dst = [sb(f"dst{i}", [P, 1], U32) for i in range(UN)]
        yb = wraw[:, :, :].rearrange("p a (n d) -> p a n d", d=P)

        s_par, s_wt, s_win, s_wst = sem("s_par"), sem("s_wt"), sem("s_win"), sem("s_wst")
        s_x = [sem(f"s_x{a}") for a in range(2)]
        s_enc = [sem(f"s_enc{a}") for a in range(2)]
        s_winb = [sem(f"s_winb{a}") for a in range(2)]
        s_wraw = [sem(f"s_wraw{a}") for a in range(2)]
        s_bias, s_fill = sem("s_bias"), sem("s_fill")
        s_scat = [sem(f"s_scat{h}") for h in range(NH)]
        s_xin = [sem(f"s_xin{a}") for a in range(UN)]
        s_yst = [sem(f"s_yst{a}") for a in range(UN)]
        s_yb = [sem(f"s_yb{a}") for a in range(2)]
        s_out = sem("s_out")
        s_cst, s_id, s_fil2 = sem("s_cst"), sem("s_id"), sem("s_fil2")
        s_w1, s_w2, s_w3, s_g = sem("s_w1"), sem("s_w2"), sem("s_w3"), sem("s_g")
        s_wT, s_wTc = sem("s_wT"), sem("s_wTc")
        s_whi, s_wlo = sem("s_whi"), sem("s_wlo")
        names = ("st1 mv1 ve1 rs1 xn st2 mv2 ve2 rs2 xm row Tenc encc Txn xnc G Gc V Vc S msk nmx exp rinv al "
                 "Tal alc O tanh x1 Txm xmc gate logc").split()
        q = {n: sem("q_" + n) for n in names}
        s_sec, s_cnt, s_rank = sem("s_sec"), sem("s_cnt"), sem("s_rank")
        s_r, s_ra, s_rp, s_route = sem("s_r"), sem("s_ra"), sem("s_rp"), sem("s_route")
        t_xT, t_xhi, t_xlo, t_up, t_pre, t_gelu = (sem("t_" + n) for n in "xT xhi xlo up pre gelu".split())
        t_hT, t_hhi, t_hlo, t_down, t_y, t_dst = (sem("t_" + n) for n in "hT hhi hlo down y dst".split())
        s_idle = sem("s_idle")
        s_f1, s_f2 = sem("s_f1"), sem("s_f2")

        block = es.enter_context(nc.Block())

        def wait(eng, s, value):
            if not (isinstance(value, int) and value <= 0):
                eng.wait_ge(s, value)

        def apart(eng):
            if eng is nc.vector:
                nc.vector.memset(idle_v[:, :], 0.0)
            else:
                nc.gpsimd.tensor_tensor(idle_p[:, :], mhalf[0:1, 0:1], mhalf[0:1, 0:1], ALU.add).then_inc(s_idle, 1)

        def live(k, r, d, n, u):
            v = r + d
            kk, rr = k + v // u, v % u
            return kk, rr, (not isinstance(kk, int)) or 0 <= kk * u + rr < n

        def tile_loop(eng, step):
            for r in range(UN):
                step(0, r)
            with eng.Fori(1, (T - 2) // UN) as k:
                for r in range(UN):
                    step(k, r)
            for u in range((T - 2) // UN * UN, T + 3):
                step(u // UN, u % UN)

        @block.sync
        def _(sp):
            sp.dma_start(ptc[:, :], pt.rearrange("(b o) -> b o", o=1)).then_inc(s_win, 16)
            sp.dma_start(lenc[:, :], lens.rearrange("(b o) -> b o", o=1)).then_inc(s_win, 16)
            sp.dma_start(xs[:, 0:GB, :], x[0:GB].rearrange("b q h -> q b h")).then_inc(s_x[0], 16)
            sp.dma_start(wa[:, :], w_a).then_inc(s_par, 16)
            sp.dma_start(wc[:, :], w_c).then_inc(s_par, 16)
            sp.dma_start(wg[:, :], w_gate).then_inc(s_par, 16)

            def load_x(k, a):
                g = 2 * k + a
                wait(sp, s_x[a], 16 * k)
                sp.dma_start(xs[:, bass.ds(GB * g, GB), :],
                             x[bass.ds(GB * g, GB)].rearrange("b q h -> q b h")).then_inc(s_x[a], 16)

            def load_ctx(k, a):
                g = 2 * k + a
                wait(sp, q["Tenc"], g - 1)
                sp.dma_start(enc[:, a], ctx_in[bass.ds(GB * g, GB)].rearrange("b l h -> l b h")).then_inc(s_enc[a], 16)
                wait(sp, q["al"], g - 1)
                sp.dma_start(win[:, a].rearrange("p b t l -> p (b t l)"),
                             win_d[bass.ds(GB * g, GB), :].rearrange("b l -> (b l)").partition_broadcast(P)
                             ).then_inc(s_winb[a], 16)

            load_x(0, 1)
            sp.wait_ge(s_g, 2)
            sp.dma_start(win_d, winall[:, :]).then_inc(s_wst, 16)
            sp.wait_ge(s_wst, 16)
            load_ctx(0, 0)
            load_x(1, 0)
            load_ctx(0, 1)
            with sp.Fori(1, NG // 2 - 1) as k:
                load_x(k, 1)
                load_ctx(k, 0)
                load_x(k + 1, 0)
                load_ctx(k, 1)
            load_x(NG // 2 - 1, 1)
            load_ctx(NG // 2 - 1, 0)
            load_ctx(NG // 2 - 1, 1)

            def load_tile(k, a):
                t = UN * k + a
                wait(sp, t_xT, t - UN + 1)
                wait(sp, t_dst, t - UN + 1)
                sp.dma_start(xin[a][:, :], slots[bass.ds(t * P, P), :]).then_inc(s_xin[a], 16)

            sp.wait_ge(s_scat[0], 16 * K * HB)
            for r in range(UN):
                load_tile(0, r)
            with sp.Fori(1, ST // UN) as k:
                for r in range(UN):
                    load_tile(k, r)
            for t in range(ST // UN * UN, ST):
                load_tile(t // UN, t % UN)
            sp.wait_ge(s_scat[1], 16 * K * HB)
            for t in range(ST, (ST // UN + 1) * UN):
                load_tile(t // UN, t % UN)
            with sp.Fori(ST // UN + 1, T // UN) as k:
                for r in range(UN):
                    load_tile(k, r)
            for t in range(T // UN * UN, T):
                load_tile(t // UN, t % UN)

            for a in range(UN):
                sp.wait_ge(s_yst[a], 16 * len(range(a, T, UN)))
            ev = eout.rearrange("(p n) d -> p n d", p=P)

            def load_y(k, a):
                g = 2 * k + a
                wait(sp, s_f2, g - 1)
                sp.dma_start(yb[:, a], ev[:, bass.ds(GB * K * g, GB * K), :]).then_inc(s_yb[a], 16)

            load_y(0, 0)
            load_y(0, 1)
            with sp.Fori(1, NG // 2) as k:
                load_y(k, 0)
                load_y(k, 1)

        @block.gpsimd
        def _(pool):
            g = nc.gpsimd
            g.iota(idx[:, :], [[1, P]], base=0, channel_multiplier=0, allow_small_or_imprecise_dtypes=True).then_inc(s_cst, 1)
            g.memset(mhalf[:, :], -0.5).then_inc(s_cst, 1)
            g.memset(epsc[:, :], EPS).then_inc(s_cst, 1)
            g.memset(ident[:, :], 0.0).then_inc(s_id, 1)
            g.memset(tri[:, :], 1.0).then_inc(s_id, 1)
            pool.wait_ge(s_id, 2)
            g.affine_select(out=ident[:, :], in_=ident[:, :], compare_op=ALU.not_equal, fill=1.0,
                            base=0, pattern=[[-1, P]], channel_multiplier=1).then_inc(s_id, 1)
            g.affine_select(out=tri[:, :], in_=tri[:, :], compare_op=ALU.is_gt, fill=0.0,
                            base=0, pattern=[[1, P]], channel_multiplier=-1).then_inc(s_id, 1)
            g.memset(neg[:, :], -1e9).then_inc(s_cst, 1)
            g.memset(ones_b[:, :], 1.0).then_inc(s_cst, 1)
            g.memset(ones8[:, :], 1.0).then_inc(s_cst, 1)
            g.iota(revidx[:, :], [[-1, E]], base=E, channel_multiplier=0, allow_small_or_imprecise_dtypes=True).then_inc(s_cst, 1)
            g.iota(caps[:, :], [[P, 16]], base=0, channel_multiplier=0, allow_small_or_imprecise_dtypes=True).then_inc(s_cst, 1)
            g.iota(tilei[:, :], [[1, ST]], base=0, channel_multiplier=0, allow_small_or_imprecise_dtypes=True).then_inc(s_cst, 1)
            g.memset(filler[:, 0:P], 0.0).then_inc(s_fil2, 1)
            g.memset(filler[:, P:ROW], SKIP).then_inc(s_fil2, 1)
            g.iota(rows[:, :, TOKEN], [[K, NB]], base=0, channel_multiplier=K * NB,
                   allow_small_or_imprecise_dtypes=True).then_inc(s_cst, 1)
            g.memset(rows[:, :, SECOND + 1:ROW], 0.0).then_inc(s_cst, 1)

            def rstd(mv, ve, rs, a, s_mv, s_ve, s_rs, n):
                pool.wait_ge(s_mv, n)
                g.tensor_tensor(ve[:, a], mv[:, a, :, 1], epsc[:, :], ALU.add).then_inc(s_ve, 1)
                pool.wait_ge(s_ve, n)
                g.tensor_tensor(rs[:, a], ve[:, a], mhalf[:, :], ALU.pow).then_inc(s_rs, 1)

            def step(k, r):
                s = 2 * k + r
                kk, a, ok = live(k, r, -2, NG, 2)
                if ok:
                    gg = 2 * kk + a
                    rstd(mv2, ve2, rs2, a, q["mv2"], q["ve2"], q["rs2"], gg + 1)
                kk, a, ok = live(k, r, 1, NG, 2)
                if ok:
                    rstd(mv1, ve1, rs1, a, q["mv1"], q["ve1"], q["rs1"], 2 * kk + a + 1)
                kk, a, ok = live(k, r, -2, NG, 2)
                if ok:
                    gg = 2 * kk + a
                    pool.wait_ge(q["xm"], gg + 1)
                    g.tensor_copy(rows[:, bass.ds(GB * gg, GB), 0:P], xm[:, a]).then_inc(q["row"], 1)

            def split(i):
                a, hi, lo = i % 2, wi_hi, wi_lo
                if i >= E * M // WCH:
                    hi, lo = wo_hi, wo_lo
                c = i % (E * M // WCH) * WCH
                pool.wait_ge(s_wraw[a], 16 * (i // 2 + 1))
                g.tensor_copy(hi[:, c:c + WCH], wraw[:, a, :]).then_inc(s_whi, 1)
                pool.wait_ge(s_whi, i + 1)
                g.tensor_tensor(lo[:, c:c + WCH], wraw[:, a, :], hi[:, c:c + WCH].bitcast(F32), ALU.subtract).then_inc(s_wlo, 1)

            def scatter(h, n0, n1):
                for n in range(n0, n1):
                    for j in range(K):
                        g.indirect_dma_start(slots, bass.IndirectOffsetOnAxis(ap=slot[:, j, n:n + 1], axis=0),
                                             rows[:, n, :], None).then_inc(s_scat[h], 16)

            rstd(mv1, ve1, rs1, 0, q["mv1"], q["ve1"], q["rs1"], 1)
            step(0, 0)
            step(0, 1)
            for i in range(2 * E * M // WCH // 2):
                split(i)
            with pool.Fori(1, 3) as k:
                step(k, 0)
                step(k, 1)
            step(3, 0)
            pool.wait_ge(s_fill, 32)
            pool.wait_ge(s_route, 1)
            pool.wait_ge(q["row"], HG)
            for i, (k, r) in enumerate(((3, 1), (4, 0), (4, 1))):
                scatter(0, 3 * i, 3 * i + 3)
                step(k, r)
            scatter(0, 9, HB)
            for i in range(2 * E * M // WCH // 2, 2 * E * M // WCH):
                split(i)
            pool.wait_ge(s_route, 2)
            pool.wait_ge(q["row"], NG)
            scatter(1, HB, NB)

            def store_y(k, r):
                kk, a, ok = live(k, r, -3, T, UN)
                if not ok:
                    return
                t = UN * kk + a
                pool.wait_ge(t_y, t + 1)
                pool.wait_ge(t_dst, t + 1)
                wait(pool, s_idle, t)
                apart(nc.gpsimd)
                g.indirect_dma_start(eout, bass.IndirectOffsetOnAxis(ap=dst[a][:, :], axis=0), ys[a][:, :], None,
                                     bounds_check=NROWS - 1, oob_is_err=False).then_inc(s_yst[a], 16)

            tile_loop(pool, store_y)

        @block.scalar
        def _(act):
            sc = nc.scalar
            def load_w(i):
                a = i % 2
                if i >= 2:
                    act.wait_ge(s_wlo, i - 1)
                    act.wait_ge(s_wraw[a], 16 * (i // 2))
                dst_w = wraw[:, a, :]
                n = WCH // M
                e0 = i % (E // n) * n
                if i < E // n:
                    act.dma_start(dst_w.rearrange("p (e m) -> p e m", e=n),
                                  w_in[e0:e0 + n].rearrange("e d m -> d e m")).then_inc(s_wraw[a], 16)
                else:
                    act.dma_start(dst_w.rearrange("p (ec d) -> p ec d", d=P),
                                  w_out[e0:e0 + n].rearrange("e (c m) d -> m (e c) d", m=P)).then_inc(s_wraw[a], 16)

            load_w(0)
            load_w(1)
            act.wait_ge(s_w3, 1)
            sc.activation(winall[:, P:2 * P], dist2[:, :], ACT.Exp, scale=-1.0 / DEV_POW).then_inc(s_g, 1)
            act.wait_ge(s_fil2, 2)
            sl = slots.rearrange("(p j) d -> p j d", p=P)
            for h in range(2):
                act.dma_start(sl[:, ST * h:ST * (h + 1), :],
                              filler[:, :].unsqueeze(1).to_broadcast([P, ST, ROW])).then_inc(s_fill, 16)
            act.dma_start(binb[:, :], b_in.rearrange("e m -> (e m)").partition_broadcast(P)).then_inc(s_bias, 16)
            act.dma_start(boutb[:, :], b_out.rearrange("e m -> (e m)").partition_broadcast(P)).then_inc(s_bias, 16)
            act.wait_ge(s_wT, 3)
            for c in range(3):
                sc.activation(waT[:, :] if c == 0 else wcT[:, c - 1, :], bank[1][:, c * P:(c + 1) * P],
                              ACT.Copy).then_inc(s_wTc, 1)

            def evac(dst_ap, src, s_in, s_done, n, s_free=None, v=0):
                act.wait_ge(s_in, n)
                if s_free is not None:
                    wait(act, s_free, v)
                sc.activation(dst_ap, src.rearrange("p (b c) -> p b c", b=GB), ACT.Copy).then_inc(s_done, 1)

            def step(k, r):
                kk, a, ok = live(k, r, -2, NG, 2)
                if ok:
                    gg = 2 * kk + a
                    act.wait_ge(q["O"], gg + 1)
                    sc.activation(p_O[:, :], p_O[:, :], ACT.Tanh).then_inc(q["tanh"], 1)
                kk, a, ok = live(k, r, 0, NG, 2)
                if ok:
                    gg = 2 * kk + a
                    evac(encT[:, :, :], p_encT[:, :], q["Tenc"], q["encc"], gg + 1, q["V"], gg)
                kk, a, ok = live(k, r, -1, NG, 2)
                if ok:
                    gg = 2 * kk + a
                    act.wait_ge(q["nmx"], gg + 1)
                    wait(act, q["al"], gg)
                    for b in range(GB):
                        ins = sc.activation(ex[:, b, :], p_S[:, b * P:(b + 1) * P], ACT.Exp, bias=nmax[:, a, b:b + 1],
                                            accum_out=ssum[:, a, b:b + 1])
                    ins.then_inc(q["exp"], 1)
                kk, a, ok = live(k, r, 0, NG, 2)
                if ok:
                    gg = 2 * kk + a
                    evac(xnT[:, a], p_xnT[:, :], q["Txn"], q["xnc"], gg + 1, q["O"], gg - 1)
                    evac(Gs[:, :, :], p_G[:, :], q["G"], q["Gc"], gg + 1, q["S"], gg)
                    evac(Vs[:, a], p_V[:, :], q["V"], q["Vc"], gg + 1, q["O"], gg - 1)
                kk, a, ok = live(k, r, -1, NG, 2)
                if ok:
                    gg = 2 * kk + a
                    evac(alT[:, :, :], p_alT[:, :], q["Tal"], q["alc"], gg + 1, q["O"], gg)
                kk, a, ok = live(k, r, -2, NG, 2)
                if ok:
                    gg = 2 * kk + a
                    evac(xmT[:, :, :], p_xmT[:, :], q["Txm"], q["xmc"], gg + 1, q["gate"], gg)
                    act.wait_ge(q["gate"], gg + 1)
                    sc.activation(logits[:, bass.ds(GB * gg, GB), :],
                                  p_log[:, 0:GB * E].rearrange("p (b e) -> p b e", b=GB), ACT.Copy).then_inc(q["logc"], 1)

            pieces = 2 * E * M // WCH
            step(0, 0)
            step(0, 1)
            for i in range(2, pieces // 2):
                load_w(i)
            with act.Fori(1, 3) as k:
                step(k, 0)
                step(k, 1)

            def gate_exp(h):
                act.wait_ge(s_ra, h + 1)
                sc.activation(me[:, :], md[:, :], ACT.Exp).then_inc(s_rp, 1)

            for k in (3, 4):
                step(k, 0)
                if k == 3:
                    gate_exp(0)
                step(k, 1)
            gate_exp(1)
            for i in range(pieces // 2, pieces):
                load_w(i)

            def tile_step(k, r):
                kk, a, ok = live(k, r, -1, T, UN)
                if ok:
                    t = UN * kk + a
                    act.wait_ge(t_pre, t + 1)
                    wait(act, t_hT, t - 1)
                    sc.activation(hid[a % 2][:, :], pre[a % 2][:, :], ACT.Gelu).then_inc(t_gelu, 1)
                    act.wait_ge(t_hT, t + 1)
                    wait(act, t_down, t - 1)
                    sc.activation(hhi[a % 2][:, :], p_hT[a % 2][:, :], ACT.Copy).then_inc(t_hhi, 1)
                kk, a, ok = live(k, r, 1, T, UN)
                if ok:
                    t = UN * kk + a
                    act.wait_ge(t_xT, t + 1)
                    wait(act, t_up, t - 1)
                    sc.activation(xhi[a % 2][:, :], p_xT[:, 0:P], ACT.Copy).then_inc(t_xhi, 1)

            act.wait_ge(t_xT, 1)
            sc.activation(xhi[0][:, :], p_xT[:, 0:P], ACT.Copy).then_inc(t_xhi, 1)
            tile_loop(act, tile_step)

            ov = out.rearrange("n q h -> q n h")

            def store(g):
                act.wait_ge(s_f2, g + 1)
                act.dma_start(ov[:, bass.ds(GB * g, GB), :], xs[:, bass.ds(GB * g, GB), :]).then_inc(s_out, 16)

            with act.Fori(0, NG) as g:
                store(g)
            act.wait_ge(s_out, 16 * NG)

        @block.vector
        def _(dve):
            v = nc.vector
            dve.wait_ge(s_win, 32)
            dve.wait_ge(s_cst, 1)
            v.tensor_copy(lenf[:, :], lenc[:, :]).then_inc(s_w1, 1)
            v.tensor_scalar(w_lo[:, :], ptc[:, :], -WINDOW, 0.0, ALU.add, ALU.max).then_inc(s_w1, 1)
            v.tensor_scalar(dist[:, :], idx[:, :], ptc[:, :], None, ALU.subtract).then_inc(s_w1, 1)
            dve.wait_ge(s_w1, 3)
            v.tensor_scalar(w_hi[:, :], ptc[:, :], WINDOW, lenf[:, :], ALU.add, ALU.min).then_inc(s_w2, 1)
            v.tensor_tensor(dist2[:, :], dist[:, :], dist[:, :], ALU.mult).then_inc(s_w3, 1)
            v.tensor_scalar(below[:, :], idx[:, :], w_lo[:, :], None, ALU.is_lt).then_inc(s_w2, 1)
            dve.wait_ge(s_w2, 2)
            v.tensor_scalar(above[:, :], idx[:, :], w_hi[:, :], None, ALU.is_gt).then_inc(s_w2, 1)
            dve.wait_ge(s_w2, 3)
            v.tensor_tensor(winall[:, 0:P], above[:, :], below[:, :], ALU.max).then_inc(s_g, 1)

            def stats(src, st, mv, a, s_st, s_mv, n):
                for b in range(GB):
                    ins = v.bn_stats(st[:, a, b, :], src(b))
                ins.then_inc(s_st, 1)
                dve.wait_ge(s_st, n)
                apart(nc.vector)
                for b in range(GB):
                    ins = v.bn_aggr(mv[:, a, b, :], st[:, a, b, :])
                ins.then_inc(s_mv, 1)

            def normalise(dstf, src, mv, rs, a, s_rs, s_done, n):
                dve.wait_ge(s_rs, n)
                for b in range(GB):
                    ins = v.tensor_scalar(dstf(b), src(b), mv[:, a, b, 0:1], rs[:, a, b:b + 1], ALU.subtract, ALU.mult)
                ins.then_inc(s_done, 1)

            def xsrc(g):
                return lambda b: xs[:, bass.ds(GB * g + b, 1), :].squeeze(1) if not isinstance(g, int) else xs[:, GB * g + b, :]

            def stats1(kk, a):
                g = 2 * kk + a
                dve.wait_ge(s_x[a], 16 * (kk + 1))
                stats(xsrc(g), st1, mv1, a, q["st1"], q["mv1"], g + 1)

            def norm1(kk, a):
                g = 2 * kk + a
                wait(dve, q["Txn"], g - 1)
                normalise(lambda b: xn[:, a, b, :], xsrc(g), mv1, rs1, a, q["rs1"], q["xn"], g + 1)

            def step(k, r):
                kk, a, ok = live(k, r, -1, NG, 2)
                if ok:
                    g = 2 * kk + a
                    dve.wait_ge(q["S"], g + 1)
                    dve.wait_ge(s_winb[a], 16 * (kk + 1))
                    apart(nc.vector)
                    sv = p_S[:, :].rearrange("p (b l) -> p b l", b=GB)
                    v.copy_predicated(sv, win[:, a, :, 0, :].bitcast(I32), neg[:, :].rearrange("p (b l) -> p b l", b=GB)
                                      ).then_inc(q["msk"], 1)
                    dve.wait_ge(q["msk"], g + 1)
                    v.tensor_reduce(nmax[:, a, :], sv, AX, ALU.max, negate=True).then_inc(q["nmx"], 1)
                kk, a, ok = live(k, r, -2, NG, 2)
                if ok:
                    g = 2 * kk + a
                    dve.wait_ge(q["tanh"], g + 1)
                    v.tensor_tensor(xs[:, bass.ds(GB * g, GB), :], p_O[:, :].rearrange("p (b h) -> p b h", b=GB),
                                    xs[:, bass.ds(GB * g, GB), :], ALU.add).then_inc(q["x1"], 1)
                    dve.wait_ge(q["x1"], g + 1)
                    apart(nc.vector)
                    stats(xsrc(g), st2, mv2, a, q["st2"], q["mv2"], g + 1)
                kk, a, ok = live(k, r, -1, NG, 2)
                if ok:
                    g = 2 * kk + a
                    dve.wait_ge(q["exp"], g + 1)
                    v.reciprocal(rinv[:, a, :], ssum[:, a, :]).then_inc(q["rinv"], 1)
                    dve.wait_ge(q["rinv"], g + 1)
                    wait(dve, q["Tal"], g)
                    for b in range(GB):
                        ins = v.scalar_tensor_tensor(al[:, b, :], ex[:, b, :], rinv[:, a, b:b + 1], win[:, a, b, 1, :],
                                                     ALU.mult, ALU.mult)
                    ins.then_inc(q["al"], 1)
                kk, a, ok = live(k, r, 1, NG, 2)
                if ok:
                    stats1(kk, a)
                kk, a, ok = live(k, r, -2, NG, 2)
                if ok:
                    g = 2 * kk + a
                    wait(dve, q["row"], g)
                    wait(dve, q["Txm"], g)
                    normalise(lambda b: xm[:, a, b, :], xsrc(g), mv2, rs2, a, q["rs2"], q["xm"], g + 1)
                kk, a, ok = live(k, r, 1, NG, 2)
                if ok:
                    norm1(kk, a)

            stats1(0, 0)
            norm1(0, 0)
            step(0, 0)
            step(0, 1)
            with dve.Fori(1, 3) as k:
                step(k, 0)
                step(k, 1)

            links = [0]

            def link(ins):
                links[0] += 1
                ins.then_inc(s_r, 1)
                dve.wait_ge(s_r, links[0])

            def wide(ap):
                return ap.unsqueeze(2).to_broadcast([P, HB, E])

            def route(h):
                dve.wait_ge(q["logc"], HG * (h + 1))
                dve.wait_ge(s_cst, 11)
                n = slice(HB * h, HB * (h + 1))
                lg = logits[:, n, :]
                rev = revidx[:, :].unsqueeze(1).to_broadcast([P, HB, E])

                def first_of(src, m, k, oh):
                    link(v.tensor_reduce(m[:, :], src, AX, ALU.max))
                    link(v.tensor_tensor(r1[:, :, :], src, wide(m[:, :]), ALU.is_equal))
                    link(v.tensor_tensor(r2[:, :, :], r1[:, :, :], rev, ALU.mult))
                    link(v.tensor_reduce(k[:, :], r2[:, :, :], AX, ALU.max))
                    link(v.tensor_tensor(oh[:, :, :], r2[:, :, :], wide(k[:, :]), ALU.is_equal))

                first_of(lg, m1, k1, oh1)
                link(v.scalar_tensor_tensor(r3[:, :, :], oh1[:, :, :], -3e38, lg, ALU.mult, ALU.add))
                first_of(r3[:, :, :], m2, k2, oh2)
                v.tensor_tensor(cnt[:, :, :], oh1[:, :, :], oh2[:, :, :], ALU.add).then_inc(s_cnt, 1)
                v.tensor_tensor(md[:, :], m2[:, :], m1[:, :], ALU.subtract).then_inc(s_ra, 1)
                v.tensor_scalar(rows[:, n, SECOND], k2[:, :], -1.0, float(E), ALU.mult, ALU.add).then_inc(s_sec, 1)

            def place(h):
                n = slice(HB * h, HB * (h + 1))
                dve.wait_ge(s_rank, h + 1)
                link(v.tensor_copy(nexp[:, :], p_cnt))
                link(v.tensor_tensor(cover[:, :, :], nexp[:, :].unsqueeze(2).to_broadcast([P, E, 16]),
                                     caps[:, :].unsqueeze(1).to_broadcast([P, E, 16]), ALU.is_gt))
                link(v.tensor_reduce(tiles_e[:, :], cover[:, :, :], AX, ALU.add))
                link(v.tensor_tensor_scan(cum[:, :], ones8[:, :], tiles_e[:, :], 0.0, ALU.mult, ALU.add))
                link(v.tensor_tensor(base[:, :], cum[:, :], tiles_e[:, :], ALU.subtract))
                link(v.tensor_scalar(nexp[:, :], base[:, :], float(P), float(P * ST * h), ALU.mult, ALU.add))
                link(v.tensor_tensor(pos[:, :, :], p_rank.rearrange("p (n e) -> p n e", e=E),
                                     nexp[:, :].unsqueeze(1).to_broadcast([P, HB, E]), ALU.add))
                link(v.tensor_tensor(r1[:, :, :], oh1[:, :, :], pos[:, :, :], ALU.mult))
                link(v.tensor_tensor(r2[:, :, :], oh2[:, :, :], pos[:, :, :], ALU.mult))
                link(v.tensor_reduce(slotf[:, 0, :], r1[:, :, :], AX, ALU.add))
                link(v.tensor_reduce(slotf[:, 1, :], r2[:, :, :], AX, ALU.add))
                link(v.tensor_copy(slot[:, :, n], slotf[:, :, :]))
                link(v.tensor_tensor(ecmp[:, :, :], cum[:, :].unsqueeze(1).to_broadcast([P, ST, E]),
                                     tilei[:, :].unsqueeze(2).to_broadcast([P, ST, E]), ALU.is_le))
                link(v.tensor_reduce(eraw[:, :], ecmp[:, :, :], AX, ALU.add))
                tt = slice(ST * h, ST * (h + 1))
                link(v.tensor_scalar(eidf[:, tt], eraw[:, :], float(E - 1), None, ALU.min))
                link(v.tensor_copy(eidi[:, tt], eidf[:, tt]))
                dve.wait_ge(s_rp, h + 1)
                link(v.tensor_scalar(md[:, :], me[:, :], 1.0, None, ALU.add))
                link(v.reciprocal(wt[:, 0, n], md[:, :]))
                v.tensor_tensor(wt[:, 1, n], me[:, :], wt[:, 0, n], ALU.mult).then_inc(s_route, 1)

            route(0)
            step(3, 0)
            place(0)
            step(3, 1)
            step(4, 0)
            step(4, 1)
            route(1)
            place(1)

            def tile_step(k, r):
                kk, a, ok = live(k, r, -3, T, UN)
                if ok:
                    t = UN * kk + a
                    dve.wait_ge(s_xin[a], 16 * (kk + 1))
                    wait(dve, s_yst[a], 16 * kk)
                    v.tensor_scalar(dst[a][:, :], xin[a][:, SECOND:SECOND + 1], eidf[:, bass.ds(t, 1)],
                                    xin[a][:, TOKEN:TOKEN + 1], ALU.is_equal, ALU.add).then_inc(t_dst, 1)
                    ev = dve.value_load(eidi[0:1, bass.ds(t, 1)], min_val=0, max_val=E - 1)
                    dve.wait_ge(t_down, t + 1)
                    v.tensor_tensor(ys[a][:, :], p_Y[:, 0:P], boutb[:, bass.ds(ev * P, P)], ALU.add).then_inc(t_y, 1)
                kk, a, ok = live(k, r, 0, T, UN)
                if ok:
                    t = UN * kk + a
                    ev = dve.value_load(eidi[0:1, bass.ds(t, 1)], min_val=0, max_val=E - 1)
                    dve.wait_ge(t_up, t + 1)
                    wait(dve, t_gelu, t - 1)
                    v.tensor_tensor(pre[a % 2][:, :], p_H[a % 2][:, :], binb[:, bass.ds(ev * M, M)], ALU.add).then_inc(t_pre, 1)
                kk, a, ok = live(k, r, -1, T, UN)
                if ok:
                    t = UN * kk + a
                    dve.wait_ge(t_hhi, t + 1)
                    v.tensor_tensor(hlo[a % 2][:, :], p_hT[a % 2][:, :], hhi[a % 2][:, :].bitcast(F32),
                                    ALU.subtract).then_inc(t_hlo, 1)
                kk, a, ok = live(k, r, 1, T, UN)
                if ok:
                    lo_x(UN * kk + a, a)

            def lo_x(t, a):
                dve.wait_ge(t_xhi, t + 1)
                v.tensor_tensor(xlo[a % 2][:, :], p_xT[:, 0:P], xhi[a % 2][:, :].bitcast(F32), ALU.subtract).then_inc(t_xlo, 1)

            dve.wait_ge(s_bias, 32)
            lo_x(0, 0)
            tile_loop(dve, tile_step)

            def combine(k, a):
                g = 2 * k + a
                dve.wait_ge(s_yb[a], 16 * (k + 1))
                for j in range(K):
                    if j:
                        dve.wait_ge(s_f1, g + 1)
                    for b in range(GB):
                        xa = xs[:, bass.ds(GB * g + b, 1), :].squeeze(1)
                        ins = v.scalar_tensor_tensor(xa, yb[:, a, K * b + j, :], wt[:, j, bass.ds(GB * g + b, 1)], xa,
                                                     ALU.mult, ALU.add)
                    ins.then_inc(s_f1 if j == 0 else s_f2, 1)

            with dve.Fori(0, NG // 2) as k:
                combine(k, 0)
                combine(k, 1)

        @block.tensor
        def _(pe):
            mm, tr = nc.tensor.matmul, nc.tensor.transpose
            pe.wait_ge(s_par, 48)
            pe.wait_ge(s_id, 4)
            for c in range(3):
                tr(bank[1][:, c * P:(c + 1) * P], wa[:, :] if c == 0 else wc[:, (c - 1) * P:c * P],
                   ident[:, :]).then_inc(s_wT, 1)
            pe.wait_ge(s_wTc, 3)

            def transpose4(dst_p, src, s):
                for b in range(GB):
                    ins = tr(dst_p[:, b * P:(b + 1) * P], src[:, b, :], ident[:, :])
                ins.then_inc(s, 1)

            def step(k, r):
                kk, a, ok = live(k, r, 0, NG, 2)
                if ok:
                    g = 2 * kk + a
                    pe.wait_ge(s_enc[a], 16 * (kk + 1))
                    wait(pe, q["Gc"], g)
                    transpose4(p_encT, enc[:, a], q["Tenc"])
                    pe.wait_ge(q["xn"], g + 1)
                    wait(pe, q["xnc"], g)
                    transpose4(p_xnT, xn[:, a], q["Txn"])
                    pe.wait_ge(q["encc"], g + 1)
                    mm(p_G[:, :], waT[:, :], encT[:, :, :].rearrange("p b l -> p (b l)"), start=True, stop=True).then_inc(q["G"], 1)
                    wait(pe, q["Vc"], g)
                    for b in range(GB):
                        ins = mm(p_V[:, b * P:(b + 1) * P], encT[:, b, :], wcT[:, 0, :], start=True, stop=True)
                    ins.then_inc(q["V"], 1)
                kk, a, ok = live(k, r, -1, NG, 2)
                if ok:
                    g = 2 * kk + a
                    pe.wait_ge(q["al"], g + 1)
                    wait(pe, q["alc"], g)
                    transpose4(p_alT, al, q["Tal"])
                kk, a, ok = live(k, r, 0, NG, 2)
                if ok:
                    g = 2 * kk + a
                    pe.wait_ge(q["xnc"], g + 1)
                    pe.wait_ge(q["Gc"], g + 1)
                    wait(pe, q["exp"], g)
                    for b in range(GB):
                        ins = mm(p_S[:, b * P:(b + 1) * P], xnT[:, a, b, :], Gs[:, b, :], start=True, stop=True)
                    ins.then_inc(q["S"], 1)
                kk, a, ok = live(k, r, -2, NG, 2)
                if ok:
                    g = 2 * kk + a
                    pe.wait_ge(q["xm"], g + 1)
                    wait(pe, q["xmc"], g)
                    transpose4(p_xmT, xm[:, a], q["Txm"])
                kk, a, ok = live(k, r, -1, NG, 2)
                if ok:
                    g = 2 * kk + a
                    pe.wait_ge(q["alc"], g + 1)
                    pe.wait_ge(q["Vc"], g + 1)
                    wait(pe, q["x1"], g)
                    for b in range(GB):
                        o = p_O[:, b * P:(b + 1) * P]
                        mm(o, xnT[:, a, b, :], wcT[:, 1, :], start=True, stop=False)
                        ins = mm(o, alT[:, b, :], Vs[:, a, b, :], start=False, stop=True)
                    ins.then_inc(q["O"], 1)
                kk, a, ok = live(k, r, -2, NG, 2)
                if ok:
                    g = 2 * kk + a
                    pe.wait_ge(q["xmc"], g + 1)
                    wait(pe, q["logc"], g)
                    if isinstance(g, int) and g == HG + 1:
                        pe.wait_ge(s_route, 1)
                    for b in range(GB):
                        ins = mm(p_log[:, b * E:(b + 1) * E], xmT[:, b, :], wg[:, :], start=True, stop=True)
                    ins.then_inc(q["gate"], 1)

            def rank(h):
                pe.wait_ge(s_cnt, h + 1)
                pe.wait_ge(q["logc"], (HG + 1, NG)[h])
                rk = p_rank.rearrange("p (n e) -> p n e", e=E)
                mm(rk, tri[:, :], cnt[:, :, :], start=True, stop=False)
                for n in range(1, HB):
                    mm(rk[:, n:HB, :], ones_b[:, :], cnt[:, 0:HB - n, :], start=False, stop=n == HB - 1)
                for n in range(HB):
                    ins = mm(p_cnt, ones_b[:, :], cnt[:, n, :], start=n == 0, stop=n == HB - 1)
                ins.then_inc(s_rank, 1)

            step(0, 0)
            step(0, 1)
            with pe.Fori(1, 3) as k:
                step(k, 0)
                step(k, 1)
            step(3, 0)
            rank(0)
            step(3, 1)
            step(4, 0)
            step(4, 1)
            rank(1)

            def x_transpose(t, kk, a):
                pe.wait_ge(s_xin[a], 16 * (kk + 1))
                wait(pe, t_xlo, t)
                tr(p_xT[:, 0:P], xin[a][:, 0:P], ident[:, :]).then_inc(t_xT, 1)

            def tile_step(k, r):
                kk, a, ok = live(k, r, 0, T, UN)
                if ok:
                    t = UN * kk + a
                    ev = pe.value_load(eidi[0:1, bass.ds(t, 1)], min_val=0, max_val=E - 1)
                    pe.wait_ge(t_xlo, t + 1)
                    wait(pe, t_pre, t - 1)
                    h = p_H[a % 2][:, :]
                    mm(h, xhi[a % 2][:, :], wi_hi[:, bass.ds(ev * M, M)], start=True, stop=False)
                    mm(h, xhi[a % 2][:, :], wi_lo[:, bass.ds(ev * M, M)], start=False, stop=False)
                    mm(h, xlo[a % 2][:, :], wi_hi[:, bass.ds(ev * M, M)], start=False, stop=True).then_inc(t_up, 1)
                kk, a, ok = live(k, r, -1, T, UN)
                if ok:
                    t = UN * kk + a
                    pe.wait_ge(t_gelu, t + 1)
                    wait(pe, t_hlo, t - 1)
                    for c in range(MC):
                        ins = tr(p_hT[a % 2][:, c * P:(c + 1) * P], hid[a % 2][:, c * P:(c + 1) * P], ident[:, :])
                    ins.then_inc(t_hT, 1)
                kk, a, ok = live(k, r, 1, T, UN)
                if ok:
                    x_transpose(UN * kk + a, kk, a)
                kk, a, ok = live(k, r, -2, T, UN)
                if ok:
                    t = UN * kk + a
                    ev = pe.value_load(eidi[0:1, bass.ds(t, 1)], min_val=0, max_val=E - 1)
                    pe.wait_ge(t_hlo, t + 1)
                    wait(pe, t_y, t)
                    y = p_Y[:, 0:P]
                    for c in range(MC):
                        hh, hl = hhi[a % 2][:, c * P:(c + 1) * P], hlo[a % 2][:, c * P:(c + 1) * P]
                        mm(y, hh, wo_hi[:, bass.ds(ev * M + c * P, P)], start=c == 0, stop=False)
                        mm(y, hh, wo_lo[:, bass.ds(ev * M + c * P, P)], start=False, stop=False)
                        ins = mm(y, hl, wo_hi[:, bass.ds(ev * M + c * P, P)], start=False, stop=c == MC - 1)
                    ins.then_inc(t_down, 1)

            pe.wait_ge(s_wlo, 2 * E * M // WCH)
            pe.wait_ge(q["Gc"], NG)
            pe.wait_ge(q["x1"], NG)
            pe.wait_ge(q["xmc"], NG)
            x_transpose(0, 0, 0)
            tile_loop(pe, tile_step)


def kernel(x, ctx_1024, condB_pt, _lenS2, L0_xcond_W_a, L0_xcond_W_c, L0_ffn_W_gate, L0_ffn_W_in, L0_ffn_b_in,
           L0_ffn_W_out, L0_ffn_b_out):
    import numpy as _np
    import concourse.bacc as _bacc
    from concourse import mybir as _mybir
    from concourse.bass_utils import run_bass_kernel_spmd as _run

    ins = dict(x=x, ctx=ctx_1024, pt=condB_pt, lens=_lenS2, w_a=L0_xcond_W_a, w_c=L0_xcond_W_c, w_gate=L0_ffn_W_gate,
               w_in=L0_ffn_W_in, b_in=L0_ffn_b_in, w_out=L0_ffn_W_out, b_out=L0_ffn_b_out)
    nc = _bacc.Bacc("TRN2", target_bir_lowering=False, num_devices=1)
    arrays, args = {}, []
    for name, a in ins.items():
        a = _np.ascontiguousarray(a)
        arrays[f"in_{name}"] = a
        args.append(nc.dram_tensor(f"in_{name}", a.shape, _mybir.dt.from_np(a.dtype), kind="ExternalInput").ap())
    o = nc.dram_tensor("out", (NB, P, P), F32, kind="ExternalOutput").ap()
    build(nc, *args, o)
    r = _run(nc, [arrays], core_ids=[0])
    return r.results[0]["out"]
```

```python
import numpy as np
import concourse.bass as bass
from concourse import mybir
from contextlib import ExitStack

F32 = mybir.dt.float32
F32R = mybir.dt.float32r
BF16 = mybir.dt.bfloat16
I32 = mybir.dt.int32
U32 = mybir.dt.uint32
U8 = mybir.dt.uint8
ALU = mybir.AluOpType
ACT = mybir.ActivationFunctionType
AX = mybir.AxisListType.X

P = 128
NB = 32
GB = 4
NG = NB // GB
NH = 2
HB = NB // NH
HG = NG // NH
E = 8
K = 2
M = 512
MC = M // P
ST = (HB * P * K + E * (P - 1)) // P
T = NH * ST
ROW = 132
TOKEN, SECOND = P, P + 1
NROWS = NB * P * K
SKIP = 65536.0
UN = 6
WCH = 512
FILLS = 3
EPS = 1e-5
WINDOW = 16.0
DEV_POW = 128.0


def build(nc, x, ctx_in, pt, lens, w_a, w_c, w_gate, w_in, b_in, w_out, b_out, out):
    slots = nc.dram_tensor("slots", [T * P, ROW], F32, kind="Internal").ap()
    eout = nc.dram_tensor("eout", [NROWS, P], F32, kind="Internal").ap()
    mask_d = nc.dram_tensor("mask_d", [NB, P], U8, kind="Internal").ap()
    gauss_d = nc.dram_tensor("gauss_d", [NB, P], F32, kind="Internal").ap()
    with ExitStack() as es:
        def sb(name, shape, dt=F32):
            return es.enter_context(nc.sbuf_tensor(name, shape, dt))

        def sem(name):
            return es.enter_context(nc.semaphore(name))

        bank = [es.enter_context(nc.psum_tensor(f"bank{i}", [P, 512], F32)) for i in range(8)]
        p_encT = p_G = bank[0]
        p_xnT, p_V, p_log, p_S, p_alT, p_O, p_xmT = bank[1], bank[2], bank[3], bank[4], bank[5], bank[6], bank[7]
        p_rank, p_cnt = bank[3][:, 128:256], bank[3][:, 256:256 + E]
        p_H, p_hT, p_xT, p_Y = [bank[0], bank[1]], [bank[4], bank[5]], bank[7], [bank[6], bank[2]]

        ident = sb("ident", [P, P])
        tri = sb("tri", [P, P], BF16)
        ones_b = sb("ones_b", [P, P], BF16)
        neg = sb("neg", [P, 512])
        mhalf, epsc, mone = sb("mhalf", [P, GB]), sb("epsc", [P, GB]), sb("mone", [P, GB])
        revidx = sb("revidx", [P, E])
        caps = sb("caps", [P, 16])
        ones8 = sb("ones8", [P, E])
        tilei = sb("tilei", [P, ST])
        filler = sb("filler", [P, ROW])
        wa, wc = sb("wa", [P, P]), sb("wc", [P, 2 * P])
        waT, wcT = sb("waT", [P, P]), sb("wcT", [P, 2, P])
        wg = sb("wg", [P, E])
        wraw = sb("wraw", [P, E * M])
        wi_hi, wi_lo = sb("wi_hi", [P, E * M], F32R), sb("wi_lo", [P, E * M], F32R)
        wo = sb("wo", [P, E * M])
        binb, boutb = sb("binb", [P, E * M]), sb("boutb", [P, E * P])
        ptc, lenc, lenf = sb("ptc", [NB, 1]), sb("lenc", [NB, 1], I32), sb("lenf", [NB, 1])
        idx = sb("idx", [NB, P])
        w_lo, w_hi = sb("w_lo", [NB, 1]), sb("w_hi", [NB, 1])
        below, dist, dist2 = sb("below", [NB, P]), sb("dist", [NB, P]), sb("dist2", [NB, P])
        above = sb("above", [NB, P])
        mask, gauss = sb("mask", [NB, P], U8), sb("gauss", [NB, P])
        xs = sb("xs", [P, NB, P])
        enc = sb("enc", [P, 2, GB, P])
        mk, gs = sb("mk", [P, 2, GB, P], U8), sb("gs", [P, 2, GB, P])
        st1, mv1 = sb("st1", [P, 2, GB, 6]), sb("mv1", [P, 2, GB, 2])
        ve1, rs1 = sb("ve1", [P, 2, GB]), sb("rs1", [P, 2, GB])
        mr1, nb1 = sb("mr1", [P, 2, GB]), sb("nb1", [P, 2, GB])
        st2, mv2 = sb("st2", [P, 2, GB, 6]), sb("mv2", [P, 2, GB, 2])
        ve2, rs2 = sb("ve2", [P, 2, GB]), sb("rs2", [P, 2, GB])
        xn, xnT = sb("xn", [P, 2, GB, P]), sb("xnT", [P, 2, GB, P])
        encT, Gs, Vs = sb("encT", [P, GB, P]), sb("Gs", [P, GB, P]), sb("Vs", [P, 2, GB, P])
        nmax, ssum, rinv = sb("nmax", [P, 2, GB]), sb("ssum", [P, 2, GB]), sb("rinv", [P, 2, GB])
        ex, al, alT = sb("ex", [P, GB, P]), sb("al", [P, GB, P]), sb("alT", [P, GB, P])
        xm, xmT = sb("xm", [P, 2, GB, P]), sb("xmT", [P, GB, P])
        rows = sb("rows", [P, NB, ROW])
        logits = sb("logits", [P, NB, E])
        idle_v, idle_p = sb("idle_v", [1, 4]), sb("idle_p", [1, 1])
        r1, r2, r3 = (sb(n, [P, HB, E]) for n in ("r1", "r2", "r3"))
        oh1, oh2 = sb("oh1", [P, HB, E]), sb("oh2", [P, HB, E])
        cnt = sb("cnt", [P, HB, E], BF16)
        m1, m2, k1, k2 = (sb(n, [P, HB]) for n in ("m1", "m2", "k1", "k2"))
        md, me, mw = (sb(n, [P, HB]) for n in ("md", "me", "mw"))
        wt = sb("wt", [P, K, NB])
        nexp, cover = sb("nexp", [P, E]), sb("cover", [P, E, 16])
        tiles_e, cum, base = sb("tiles_e", [P, E]), sb("cum", [P, E]), sb("base", [P, E])
        pos = sb("pos", [P, HB, E])
        slotf, slot = sb("slotf", [P, K, HB]), sb("slot", [P, K, NB], U32)
        ecmp, eraw = sb("ecmp", [P, ST, E]), sb("eraw", [P, ST])
        eidf, eidi = sb("eidf", [P, T]), sb("eidi", [P, T], I32)
        xin = [sb(f"xin{i}", [P, ROW]) for i in range(UN)]
        xhi = [sb(f"xhi{i}", [P, P], F32R) for i in range(2)]
        xlo = [sb(f"xlo{i}", [P, P], F32R) for i in range(2)]
        pre = [sb(f"pre{i}", [P, M]) for i in range(2)]
        hid = [sb(f"hid{i}", [P, M]) for i in range(2)]
        hT = [sb(f"hT{i}", [P, M]) for i in range(2)]
        ys = [sb(f"ys{i}", [P, P]) for i in range(UN)]
        dst = [sb(f"dst{i}", [P, 1], U32) for i in range(UN)]
        yb = wraw[:, :].rearrange("p (a n d) -> p a n d", a=HG, d=P)

        s_par, s_win, s_wst, s_wo = sem("s_par"), sem("s_win"), sem("s_wst"), sem("s_wo")
        s_x = [sem(f"s_x{a}") for a in range(2)]
        s_enc = [sem(f"s_enc{a}") for a in range(2)]
        s_winb = [sem(f"s_winb{a}") for a in range(2)]
        s_wraw = sem("s_wraw")
        s_bias = sem("s_bias")
        s_fill = [sem(f"s_fill{h}") for h in range(NH)]
        s_scat = [sem(f"s_scat{h}") for h in range(NH)]
        s_xin = [sem(f"s_xin{a}") for a in range(UN)]
        s_yst = [sem(f"s_yst{a}") for a in range(UN)]
        s_yb = [sem(f"s_yb{a}") for a in range(HG)]
        s_out, s_out0 = sem("s_out"), sem("s_out0")
        s_cst, s_id, s_fil2 = sem("s_cst"), sem("s_id"), sem("s_fil2")
        s_w1, s_w2, s_w3, s_g = sem("s_w1"), sem("s_w2"), sem("s_w3"), sem("s_g")
        s_wT, s_wTc = sem("s_wT"), sem("s_wTc")
        s_whi, s_wlo = sem("s_whi"), sem("s_wlo")
        names = ("st1 mv1 ve1 rs1 mr1 nb1 xn st2 mv2 ve2 rs2 xm row Tenc encc Txn xnc G Gc V Vc S msk nmx exp rinv al "
                 "Tal alc O tanh x1 Txm xmc gate logc").split()
        q = {n: sem("q_" + n) for n in names}
        s_sec, s_cnt, s_rank = sem("s_sec"), sem("s_cnt"), sem("s_rank")
        s_r, s_ra, s_rp, s_route = sem("s_r"), sem("s_ra"), sem("s_rp"), sem("s_route")
        t_xT, t_xhi, t_xlo, t_up, t_pre, t_gelu = (sem("t_" + n) for n in "xT xhi xlo up pre gelu".split())
        t_hT, t_hc, t_down, t_y, t_dst = (sem("t_" + n) for n in "hT hc down y dst".split())
        s_idle, s_rows = sem("s_idle"), sem("s_rows")
        s_f1, s_f2 = sem("s_f1"), sem("s_f2")

        ov = out.rearrange("n q h -> q n h")
        block = es.enter_context(nc.Block())

        def wait(eng, s, value):
            if not (isinstance(value, int) and value <= 0):
                eng.wait_ge(s, value)

        def apart(eng, cell=0):
            if eng is nc.vector:
                nc.vector.memset(idle_v[:, cell:cell + 1], 0.0)
            else:
                nc.gpsimd.tensor_tensor(idle_p[:, :], mhalf[0:1, 0:1], mhalf[0:1, 0:1], ALU.add).then_inc(s_idle, 1)

        def live(k, r, d, n, u):
            v = r + d
            kk, rr = k + v // u, v % u
            return kk, rr, (not isinstance(kk, int)) or 0 <= kk * u + rr < n

        turns = (T - 2 * UN - 1) // UN

        def tile_loop(eng, step, late=None):
            for u in range(2 * UN - 1):
                step(u // UN, u % UN)
            split_at = 1 + turns - HG if late else 1 + turns
            with eng.Fori(1, split_at) as k:
                for r in range(UN - 1, 2 * UN - 1):
                    step(k + r // UN, r % UN)
            if late:
                with eng.Fori(split_at, 1 + turns) as k:
                    for i, r in enumerate(range(UN - 1, 2 * UN - 1)):
                        step(k + r // UN, r % UN)
                        late(k - split_at, i)
            for u in range(2 * UN - 1 + turns * UN, T + 3):
                step(u // UN, u % UN)

        @block.sync
        def _(sp):
            sp.dma_start(ptc[:, :], pt.rearrange("(b o) -> b o", o=1)).then_inc(s_win, 16)
            sp.dma_start(lenc[:, :], lens.rearrange("(b o) -> b o", o=1)).then_inc(s_win, 16)

            def load_x(k, a):
                g = 2 * k + a
                wait(sp, s_x[a], 16 * k)
                sp.dma_start(xs[:, bass.ds(GB * g, GB), :],
                             x[bass.ds(GB * g, GB)].rearrange("b q h -> q b h")).then_inc(s_x[a], 16)

            def load_ctx(k, a):
                g = 2 * k + a
                wait(sp, q["Tenc"], g - 1)
                sp.dma_start(enc[:, a], ctx_in[bass.ds(GB * g, GB)].rearrange("b l h -> l b h")).then_inc(s_enc[a], 16)

            def load_window(k, a):
                g = 2 * k + a
                wait(sp, q["al"], g - 1)
                sp.dma_start(mk[:, a].rearrange("p b l -> p (b l)"),
                             mask_d[bass.ds(GB * g, GB), :].rearrange("b l -> (b l)").partition_broadcast(P)
                             ).then_inc(s_winb[a], 16)
                sp.dma_start(gs[:, a].rearrange("p b l -> p (b l)"),
                             gauss_d[bass.ds(GB * g, GB), :].rearrange("b l -> (b l)").partition_broadcast(P)
                             ).then_inc(s_winb[a], 16)

            def copy_rows(k, a):
                g = 2 * k + a
                sp.wait_ge(q["xm"], g + 1)
                sp.dma_start(rows[:, bass.ds(GB * g, GB), 0:P], xm[:, a]).then_inc(s_rows, 16)
                sp.wait_ge(s_rows, 16 * (g + 1))

            load_x(0, 0)
            load_ctx(0, 0)
            sp.dma_start(wa[:, :], w_a).then_inc(s_par, 16)
            sp.dma_start(wc[:, :], w_c).then_inc(s_par, 16)
            sp.dma_start(wg[:, :], w_gate).then_inc(s_par, 16)
            load_x(0, 1)
            sp.wait_ge(s_g, 2)
            sp.dma_start(mask_d, mask[:, :]).then_inc(s_wst, 16)
            sp.dma_start(gauss_d, gauss[:, :]).then_inc(s_wst, 16)
            sp.wait_ge(s_wst, 32)
            load_window(0, 0)
            load_ctx(0, 1)
            load_x(1, 0)
            load_window(0, 1)
            load_x(1, 1)
            load_ctx(1, 0)
            load_x(2, 0)
            load_window(1, 0)

            def step(k, r):
                kk, a, ok = live(k, r, 1, NG, 2)
                if ok:
                    load_ctx(kk, a)
                kk, a, ok = live(k, r, 1, NG, 2)
                if ok:
                    load_window(kk, a)
                kk, a, ok = live(k, r, -2, NG, 2)
                if ok:
                    copy_rows(kk, a)
                kk, a, ok = live(k, r, 3, NG, 2)
                if ok:
                    load_x(kk, a)

            step(1, 0)
            with sp.Fori(1, 2) as k:
                step(k, 1)
                step(k + 1, 0)
            for st in range(5, NG + 2):
                step(st // 2, st % 2)

            def load_tile(k, a):
                t = UN * k + a
                wait(sp, t_xT, t - UN + 1)
                wait(sp, t_dst, t - UN + 1)
                sp.dma_start(xin[a][:, :], slots[bass.ds(t * P, P), :]).then_inc(s_xin[a], 16)

            sp.wait_ge(s_scat[0], 16 * K * HB)
            for r in range(UN):
                load_tile(0, r)
            with sp.Fori(1, ST // UN) as k:
                for r in range(UN):
                    load_tile(k, r)
            for t in range(ST // UN * UN, ST):
                load_tile(t // UN, t % UN)
            sp.wait_ge(s_scat[1], 16 * K * HB)
            for t in range(ST, (ST // UN + 1) * UN):
                load_tile(t // UN, t % UN)
            k0 = T // UN - HG - 1
            with sp.Fori(ST // UN + 1, k0) as k:
                for r in range(UN):
                    load_tile(k, r)

            ev = eout.rearrange("(p n) d -> p n d", p=P)

            def load_y(g, a):
                sp.dma_start(yb[:, a], ev[:, GB * K * g:GB * K * (g + 1), :]).then_inc(s_yb[a], 16)

            for a in range(UN):
                sp.wait_ge(s_yst[a], 16 * len(range(a, ST, UN)))
            for g in range(HG):
                load_y(g, g)
            with sp.Fori(k0, T // UN) as k:
                for r in range(UN):
                    load_tile(k, r)
            for t in range(T // UN * UN, T):
                load_tile(t // UN, t % UN)
            sp.wait_ge(s_f2, HG)
            sp.dma_start(ov[:, 0:HB, :], xs[:, 0:HB, :]).then_inc(s_out0, 16)
            for a in range(UN):
                sp.wait_ge(s_yst[a], 16 * len(range(a, T, UN)))
            for g in range(HG, NG):
                load_y(g, g - HG)
            sp.wait_ge(s_out0, 16)

        @block.gpsimd
        def _(pool):
            g = nc.gpsimd
            g.iota(idx[:, :], [[1, P]], base=0, channel_multiplier=0, allow_small_or_imprecise_dtypes=True).then_inc(s_cst, 1)
            g.memset(mhalf[:, :], -0.5).then_inc(s_cst, 1)
            g.memset(epsc[:, :], EPS).then_inc(s_cst, 1)
            g.memset(mone[:, :], -1.0).then_inc(s_cst, 1)
            g.memset(ident[:, :], 0.0).then_inc(s_id, 1)
            g.memset(tri[:, :], 1.0).then_inc(s_id, 1)
            pool.wait_ge(s_id, 2)
            g.affine_select(out=ident[:, :], in_=ident[:, :], compare_op=ALU.not_equal, fill=1.0,
                            base=0, pattern=[[-1, P]], channel_multiplier=1).then_inc(s_id, 1)
            g.affine_select(out=tri[:, :], in_=tri[:, :], compare_op=ALU.is_gt, fill=0.0,
                            base=0, pattern=[[1, P]], channel_multiplier=-1).then_inc(s_id, 1)
            g.memset(neg[:, :], -1e9).then_inc(s_cst, 1)
            g.memset(ones_b[:, :], 1.0).then_inc(s_cst, 1)
            g.memset(ones8[:, :], 1.0).then_inc(s_cst, 1)
            g.iota(revidx[:, :], [[-1, E]], base=E, channel_multiplier=0, allow_small_or_imprecise_dtypes=True).then_inc(s_cst, 1)
            g.iota(caps[:, :], [[P, 16]], base=0, channel_multiplier=0, allow_small_or_imprecise_dtypes=True).then_inc(s_cst, 1)
            g.iota(tilei[:, :], [[1, ST]], base=0, channel_multiplier=0, allow_small_or_imprecise_dtypes=True).then_inc(s_cst, 1)
            g.memset(filler[:, 0:P], 0.0).then_inc(s_fil2, 1)
            g.memset(filler[:, P:ROW], SKIP).then_inc(s_fil2, 1)
            g.iota(rows[:, :, TOKEN], [[K, NB]], base=0, channel_multiplier=K * NB,
                   allow_small_or_imprecise_dtypes=True).then_inc(s_cst, 1)
            g.memset(rows[:, :, SECOND + 1:ROW], 0.0).then_inc(s_cst, 1)

            def rstd(mv, ve, rs, a, s_mv, s_ve, s_rs, n):
                pool.wait_ge(s_mv, n)
                g.tensor_tensor(ve[:, a], mv[:, a, :, 1], epsc[:, :], ALU.add).then_inc(s_ve, 1)
                pool.wait_ge(s_ve, n)
                g.tensor_tensor(rs[:, a], ve[:, a], mhalf[:, :], ALU.pow).then_inc(s_rs, 1)

            def rstd1(kk, a):
                n = 2 * kk + a + 1
                rstd(mv1, ve1, rs1, a, q["mv1"], q["ve1"], q["rs1"], n)
                pool.wait_ge(q["rs1"], n)
                g.tensor_tensor(mr1[:, a], mv1[:, a, :, 0], rs1[:, a], ALU.mult).then_inc(q["mr1"], 1)
                pool.wait_ge(q["mr1"], n)
                g.tensor_tensor(nb1[:, a], mr1[:, a], mone[:, :], ALU.mult).then_inc(q["nb1"], 1)

            def step(k, r):
                kk, a, ok = live(k, r, -2, NG, 2)
                if ok:
                    rstd(mv2, ve2, rs2, a, q["mv2"], q["ve2"], q["rs2"], 2 * kk + a + 1)
                kk, a, ok = live(k, r, 2, NG, 2)
                if ok:
                    rstd1(kk, a)

            def split(k, a):
                i = 2 * k + a
                raw = wraw[:, bass.ds(i * WCH, WCH)]
                hi = wi_hi[:, bass.ds(i * WCH, WCH)]
                g.tensor_copy(hi, raw).then_inc(s_whi, 1)
                pool.wait_ge(s_whi, i + 1)
                g.tensor_tensor(wi_lo[:, bass.ds(i * WCH, WCH)], raw, hi.bitcast(F32), ALU.subtract).then_inc(s_wlo, 1)

            def scatter(h, n0, n1):
                for n in range(n0, n1):
                    for j in range(K):
                        g.indirect_dma_start(slots, bass.IndirectOffsetOnAxis(ap=slot[:, j, n:n + 1], axis=0),
                                             rows[:, n, :], None).then_inc(s_scat[h], 16)

            rstd1(0, 0)
            rstd1(0, 1)
            step(0, 0)
            step(0, 1)
            pool.wait_ge(s_wraw, 16)
            with pool.Fori(1, 3) as k:
                step(k, 0)
                split(k - 1, 0)
                step(k, 1)
                split(k - 1, 1)
            step(3, 0)
            split(2, 0)
            pool.wait_ge(s_fill[0], 16 * FILLS)
            pool.wait_ge(s_route, 1)
            pool.wait_ge(s_rows, 16 * HG)
            for i, (k, r) in enumerate(((3, 1), (4, 0), (4, 1))):
                scatter(0, i, i + 1)
                step(k, r)
                split(k - 1, r)
            scatter(0, 3, HB)
            pool.wait_ge(s_fill[1], 16 * FILLS)
            pool.wait_ge(s_route, 2)
            pool.wait_ge(s_rows, 16 * NG)

            def store_y(k, r):
                kk, a, ok = live(k, r, -3, T, UN)
                if not ok:
                    return
                t = UN * kk + a
                pool.wait_ge(t_y, t + 1)
                pool.wait_ge(t_dst, t + 1)
                wait(pool, s_idle, t)
                apart(nc.gpsimd)
                g.indirect_dma_start(eout, bass.IndirectOffsetOnAxis(ap=dst[a][:, :], axis=0), ys[a][:, :], None,
                                     bounds_check=NROWS - 1, oob_is_err=False).then_inc(s_yst[a], 16)

            for i in range(HB):
                scatter(1, HB + i, HB + i + 1)
                for t in (2 * i, 2 * i + 1):
                    store_y((t + 3) // UN, (t + 3) % UN)
            t0 = 2 * HB // UN * UN + UN
            for t in range(2 * HB, t0):
                store_y((t + 3) // UN, (t + 3) % UN)
            turns = (T - t0) // UN
            with pool.Fori(t0 // UN, t0 // UN + turns) as k:
                for r in range(UN):
                    store_y(k + (r + 3) // UN, (r + 3) % UN)
            for t in range(t0 + turns * UN, T):
                store_y((t + 3) // UN, (t + 3) % UN)

        @block.scalar
        def _(act):
            sc = nc.scalar
            def fill(h, i):
                n = ST // FILLS
                act.dma_start(slots.rearrange("(h i p j) d -> h i p j d", h=NH, i=FILLS, p=P)[h, i],
                              filler[:, :].unsqueeze(1).to_broadcast([P, n, ROW])).then_inc(s_fill[h], 16)

            def load_wo(i):
                n = E // 4
                act.dma_start(wo[:, i * n * M:(i + 1) * n * M].rearrange("p (ec d) -> p ec d", d=P),
                              w_out[i * n:(i + 1) * n].rearrange("e (c m) d -> m (e c) d", m=P)).then_inc(s_wo, 16)

            act.wait_ge(s_w3, 1)
            sc.activation(gauss[:, :], dist2[:, :], ACT.Exp, scale=-1.0 / DEV_POW).then_inc(s_g, 1)
            act.wait_ge(s_wT, 3)
            for c in range(3):
                sc.activation(waT[:, :] if c == 0 else wcT[:, c - 1, :], bank[1][:, c * P:(c + 1) * P],
                              ACT.Copy).then_inc(s_wTc, 1)

            def evac(dst_ap, src, s_in, s_done, n):
                act.wait_ge(s_in, n)
                sc.activation(dst_ap, src.rearrange("p (b c) -> p b c", b=GB), ACT.Copy).then_inc(s_done, 1)

            def norm1(kk, a):
                g = 2 * kk + a
                act.wait_ge(q["nb1"], g + 1)
                for b in range(GB):
                    ins = sc.activation(xn[:, a, b, :], xs[:, bass.ds(GB * g + b, 1), :].squeeze(1), ACT.Identity,
                                        scale=rs1[:, a, b:b + 1], bias=nb1[:, a, b:b + 1])
                ins.then_inc(q["xn"], 1)

            def step(k, r):
                k0, a0, ok0 = live(k, r, 0, NG, 2)
                k1, a1, ok1 = live(k, r, -1, NG, 2)
                k2, a2, ok2 = live(k, r, -2, NG, 2)
                kn, an, okn = live(k, r, 1, NG, 2)
                g0, g1, g2 = 2 * k0 + a0, 2 * k1 + a1, 2 * k2 + a2
                if ok0:
                    evac(encT[:, :, :], p_encT[:, :], q["Tenc"], q["encc"], g0 + 1)
                    evac(xnT[:, a0], p_xnT[:, :], q["Txn"], q["xnc"], g0 + 1)
                    evac(Gs[:, :, :], p_G[:, :], q["G"], q["Gc"], g0 + 1)
                    evac(Vs[:, a0], p_V[:, :], q["V"], q["Vc"], g0 + 1)
                if ok1:
                    evac(alT[:, :, :], p_alT[:, :], q["Tal"], q["alc"], g1 + 1)
                if okn:
                    norm1(kn, an)
                if ok1:
                    act.wait_ge(q["O"], g1 + 1)
                    sc.activation(p_O[:, :], p_O[:, :], ACT.Tanh).then_inc(q["tanh"], 1)
                if ok2:
                    evac(xmT[:, :, :], p_xmT[:, :], q["Txm"], q["xmc"], g2 + 1)
                if ok0:
                    act.wait_ge(q["nmx"], g0 + 1)
                    for b in range(GB):
                        ins = sc.activation(ex[:, b, :], p_S[:, b * P:(b + 1) * P], ACT.Exp, bias=nmax[:, a0, b:b + 1],
                                            accum_out=ssum[:, a0, b:b + 1])
                    ins.then_inc(q["exp"], 1)
                if ok2:
                    act.wait_ge(q["gate"], g2 + 1)
                    sc.activation(logits[:, bass.ds(GB * g2, GB), :],
                                  p_log[:, 0:GB * E].rearrange("p (b e) -> p b e", b=GB), ACT.Copy).then_inc(q["logc"], 1)

            def gate_exp(h):
                act.wait_ge(s_ra, h + 1)
                sc.activation(me[:, :], md[:, :], ACT.Exp).then_inc(s_rp, 1)

            norm1(0, 0)
            step(0, 0)
            act.dma_start(wraw[:, :].rearrange("p (e m) -> p e m", e=E), w_in.rearrange("e d m -> d e m")).then_inc(s_wraw, 16)
            step(0, 1)
            act.wait_ge(s_fil2, 2)
            fill(0, 0)
            fill(0, 1)
            with act.Fori(1, 3) as k:
                step(k, 0)
                step(k, 1)
            fill(0, 2)
            load_wo(0)
            step(3, 0)
            gate_exp(0)
            for i in range(FILLS):
                fill(1, i)
            load_wo(1)
            step(3, 1)
            load_wo(2)
            load_wo(3)
            step(4, 0)
            act.dma_start(binb[:, :], b_in.rearrange("e m -> (e m)").partition_broadcast(P)).then_inc(s_bias, 16)
            act.dma_start(boutb[:, :], b_out.rearrange("e m -> (e m)").partition_broadcast(P)).then_inc(s_bias, 16)
            step(4, 1)
            gate_exp(1)

            def hi_x(t, a):
                act.wait_ge(t_xT, t + 1)
                sc.activation(xhi[a % 2][:, :], p_xT[:, 0:P], ACT.Copy).then_inc(t_xhi, 1)

            def tile_step(k, r):
                kk, a, ok = live(k, r, -1, T, UN)
                if ok:
                    t = UN * kk + a
                    act.wait_ge(t_hT, t + 1)
                    wait(act, t_down, t - 1)
                    sc.activation(hT[a % 2][:, :], p_hT[a % 2][:, :], ACT.Copy).then_inc(t_hc, 1)
                kk, a, ok = live(k, r, 0, T, UN)
                if ok:
                    act.wait_ge(t_pre, UN * kk + a + 1)
                    sc.activation(hid[a % 2][:, :], pre[a % 2][:, :], ACT.Gelu).then_inc(t_gelu, 1)
                kk, a, ok = live(k, r, 2, T, UN)
                if ok:
                    hi_x(UN * kk + a, a)

            hi_x(0, 0)
            hi_x(1, 1)
            tile_loop(act, tile_step)

            with act.Fori(HG, NG) as g:
                act.wait_ge(s_f2, g + 1)
                act.dma_start(ov[:, bass.ds(GB * g, GB), :], xs[:, bass.ds(GB * g, GB), :]).then_inc(s_out, 16)
            act.wait_ge(s_out, 16 * HG)

        @block.vector
        def _(dve):
            v = nc.vector
            dve.wait_ge(s_win, 32)
            dve.wait_ge(s_cst, 1)
            v.tensor_copy(lenf[:, :], lenc[:, :]).then_inc(s_w1, 1)
            v.tensor_scalar(w_lo[:, :], ptc[:, :], -WINDOW, 0.0, ALU.add, ALU.max).then_inc(s_w1, 1)
            v.tensor_scalar(dist[:, :], idx[:, :], ptc[:, :], None, ALU.subtract).then_inc(s_w1, 1)
            dve.wait_ge(s_w1, 3)
            v.tensor_scalar(w_hi[:, :], ptc[:, :], WINDOW, lenf[:, :], ALU.add, ALU.min).then_inc(s_w2, 1)
            v.tensor_tensor(dist2[:, :], dist[:, :], dist[:, :], ALU.mult).then_inc(s_w3, 1)
            v.tensor_scalar(below[:, :], idx[:, :], w_lo[:, :], None, ALU.is_lt).then_inc(s_w2, 1)
            dve.wait_ge(s_w2, 2)
            v.tensor_scalar(above[:, :], idx[:, :], w_hi[:, :], None, ALU.is_gt).then_inc(s_w2, 1)
            dve.wait_ge(s_w2, 3)
            v.tensor_tensor(mask[:, :], above[:, :], below[:, :], ALU.max).then_inc(s_g, 1)

            def stats(src, st, mv, a, s_st, s_mv, n):
                for b in range(GB):
                    ins = v.bn_stats(st[:, a, b, :], src(b))
                ins.then_inc(s_st, 1)
                dve.wait_ge(s_st, n)
                apart(nc.vector, 2 if st is st1 else 3)
                for b in range(GB):
                    ins = v.bn_aggr(mv[:, a, b, :], st[:, a, b, :])
                ins.then_inc(s_mv, 1)

            def normalise(dstf, src, mv, rs, a, s_rs, s_done, n):
                dve.wait_ge(s_rs, n)
                for b in range(GB):
                    ins = v.tensor_scalar(dstf(b), src(b), mv[:, a, b, 0:1], rs[:, a, b:b + 1], ALU.subtract, ALU.mult)
                ins.then_inc(s_done, 1)

            def xsrc(g):
                return lambda b: xs[:, bass.ds(GB * g + b, 1), :].squeeze(1) if not isinstance(g, int) else xs[:, GB * g + b, :]

            def stats1(kk, a):
                g = 2 * kk + a
                dve.wait_ge(s_x[a], 16 * (kk + 1))
                stats(xsrc(g), st1, mv1, a, q["st1"], q["mv1"], g + 1)

            def step(k, r):
                k0, a0, ok0 = live(k, r, 0, NG, 2)
                k1, a1, ok1 = live(k, r, -1, NG, 2)
                k2, a2, ok2 = live(k, r, -2, NG, 2)
                kn, an, okn = live(k, r, 2, NG, 2)
                g0, g1, g2 = 2 * k0 + a0, 2 * k1 + a1, 2 * k2 + a2
                if ok2:
                    dve.wait_ge(q["tanh"], g2 + 1)
                    v.tensor_tensor(xs[:, bass.ds(GB * g2, GB), :], p_O[:, :].rearrange("p (b h) -> p b h", b=GB),
                                    xs[:, bass.ds(GB * g2, GB), :], ALU.add).then_inc(q["x1"], 1)
                    dve.wait_ge(q["x1"], g2 + 1)
                    apart(nc.vector, 0)
                    stats(xsrc(g2), st2, mv2, a2, q["st2"], q["mv2"], g2 + 1)
                if ok1:
                    dve.wait_ge(q["exp"], g1 + 1)
                    v.reciprocal(rinv[:, a1, :], ssum[:, a1, :]).then_inc(q["rinv"], 1)
                    dve.wait_ge(q["rinv"], g1 + 1)
                    for b in range(GB):
                        ins = v.scalar_tensor_tensor(al[:, b, :], ex[:, b, :], rinv[:, a1, b:b + 1], gs[:, a1, b, :],
                                                     ALU.mult, ALU.mult)
                    ins.then_inc(q["al"], 1)
                if ok2:
                    if isinstance(g2, int):
                        wait(dve, s_rows, 16 * (g2 - 1))
                    normalise(lambda b: xm[:, a2, b, :], xsrc(g2), mv2, rs2, a2, q["rs2"], q["xm"], g2 + 1)
                if ok0:
                    dve.wait_ge(q["S"], g0 + 1)
                    dve.wait_ge(s_winb[a0], 32 * (k0 + 1))
                    apart(nc.vector, 1)
                    sv = p_S[:, :].rearrange("p (b l) -> p b l", b=GB)
                    v.copy_predicated(sv, mk[:, a0], neg[:, :].rearrange("p (b l) -> p b l", b=GB)).then_inc(q["msk"], 1)
                    dve.wait_ge(q["msk"], g0 + 1)
                    v.tensor_reduce(nmax[:, a0, :], sv, AX, ALU.max, negate=True).then_inc(q["nmx"], 1)
                if okn:
                    stats1(kn, an)

            stats1(0, 0)
            stats1(0, 1)
            step(0, 0)
            step(0, 1)
            with dve.Fori(1, 3) as k:
                step(k, 0)
                step(k, 1)

            links = [0]

            def link(ins):
                links[0] += 1
                ins.then_inc(s_r, 1)
                dve.wait_ge(s_r, links[0])

            def wide(ap):
                return ap.unsqueeze(2).to_broadcast([P, HB, E])

            def route(h):
                dve.wait_ge(q["logc"], HG * (h + 1))
                dve.wait_ge(s_cst, 12)
                n = slice(HB * h, HB * (h + 1))
                lg = logits[:, n, :]
                rev = revidx[:, :].unsqueeze(1).to_broadcast([P, HB, E])

                def first_of(src, m, k, oh):
                    link(v.tensor_reduce(m[:, :], src, AX, ALU.max))
                    link(v.tensor_tensor(r1[:, :, :], src, wide(m[:, :]), ALU.is_equal))
                    link(v.tensor_tensor(r2[:, :, :], r1[:, :, :], rev, ALU.mult))
                    link(v.tensor_reduce(k[:, :], r2[:, :, :], AX, ALU.max))
                    link(v.tensor_tensor(oh[:, :, :], r2[:, :, :], wide(k[:, :]), ALU.is_equal))

                first_of(lg, m1, k1, oh1)
                link(v.scalar_tensor_tensor(r3[:, :, :], oh1[:, :, :], -3e38, lg, ALU.mult, ALU.add))
                first_of(r3[:, :, :], m2, k2, oh2)
                v.tensor_tensor(cnt[:, :, :], oh1[:, :, :], oh2[:, :, :], ALU.add).then_inc(s_cnt, 1)
                v.tensor_tensor(md[:, :], m2[:, :], m1[:, :], ALU.subtract).then_inc(s_ra, 1)
                v.tensor_scalar(rows[:, n, SECOND], k2[:, :], -1.0, float(E), ALU.mult, ALU.add).then_inc(s_sec, 1)

            def place(h):
                n = slice(HB * h, HB * (h + 1))
                dve.wait_ge(s_rank, h + 1)
                link(v.tensor_copy(nexp[:, :], p_cnt))
                link(v.tensor_tensor(cover[:, :, :], nexp[:, :].unsqueeze(2).to_broadcast([P, E, 16]),
                                     caps[:, :].unsqueeze(1).to_broadcast([P, E, 16]), ALU.is_gt))
                link(v.tensor_reduce(tiles_e[:, :], cover[:, :, :], AX, ALU.add))
                link(v.tensor_tensor_scan(cum[:, :], ones8[:, :], tiles_e[:, :], 0.0, ALU.mult, ALU.add))
                link(v.tensor_tensor(base[:, :], cum[:, :], tiles_e[:, :], ALU.subtract))
                link(v.tensor_scalar(nexp[:, :], base[:, :], float(P), float(P * ST * h), ALU.mult, ALU.add))
                link(v.tensor_tensor(pos[:, :, :], p_rank.rearrange("p (n e) -> p n e", e=E),
                                     nexp[:, :].unsqueeze(1).to_broadcast([P, HB, E]), ALU.add))
                link(v.tensor_tensor(r1[:, :, :], oh1[:, :, :], pos[:, :, :], ALU.mult))
                link(v.tensor_tensor(r2[:, :, :], oh2[:, :, :], pos[:, :, :], ALU.mult))
                link(v.tensor_reduce(slotf[:, 0, :], r1[:, :, :], AX, ALU.add))
                link(v.tensor_reduce(slotf[:, 1, :], r2[:, :, :], AX, ALU.add))
                link(v.tensor_copy(slot[:, :, n], slotf[:, :, :]))
                link(v.tensor_tensor(ecmp[:, :, :], cum[:, :].unsqueeze(1).to_broadcast([P, ST, E]),
                                     tilei[:, :].unsqueeze(2).to_broadcast([P, ST, E]), ALU.is_le))
                link(v.tensor_reduce(eraw[:, :], ecmp[:, :, :], AX, ALU.add))
                tt = slice(ST * h, ST * (h + 1))
                link(v.tensor_scalar(eidf[:, tt], eraw[:, :], float(E - 1), None, ALU.min))
                link(v.tensor_copy(eidi[:, tt], eidf[:, tt]))
                dve.wait_ge(s_rp, h + 1)
                link(v.tensor_scalar(md[:, :], me[:, :], 1.0, None, ALU.add))
                link(v.reciprocal(wt[:, 0, n], md[:, :]))
                v.tensor_tensor(wt[:, 1, n], me[:, :], wt[:, 0, n], ALU.mult).then_inc(s_route, 1)

            route(0)
            step(3, 0)
            place(0)
            step(3, 1)
            step(4, 0)
            step(4, 1)
            route(1)
            place(1)

            def load_expert(kk, a):
                dve.reg_load(expert[a], eidi[0:1, bass.ds(UN * kk + a, 1)])

            def tile_step(k, r):
                kk, a, ok = live(k, r, -3, T, UN)
                if ok:
                    t = UN * kk + a
                    ev = dve.snap(expert[a], min_val=0, max_val=E - 1)
                    dve.wait_ge(t_down, t + 1)
                    v.tensor_tensor(ys[a][:, :], p_Y[a % 2][:, 0:P], boutb[:, bass.ds(ev * P, P)], ALU.add).then_inc(t_y, 1)
                kk, a, ok = live(k, r, 0, T, UN)
                if ok:
                    t = UN * kk + a
                    ev = dve.snap(expert[a], min_val=0, max_val=E - 1)
                    dve.wait_ge(t_up, t + 1)
                    wait(dve, t_gelu, t - 1)
                    v.tensor_tensor(pre[a % 2][:, :], p_H[a % 2][:, :], binb[:, bass.ds(ev * M, M)], ALU.add).then_inc(t_pre, 1)
                kk, a, ok = live(k, r, 1, T, UN)
                if ok:
                    load_expert(kk, a)
                kk, a, ok = live(k, r, 0, T, UN)
                if ok:
                    t = UN * kk + a
                    wait(dve, s_yst[a], 16 * kk)
                    v.tensor_scalar(dst[a][:, :], xin[a][:, SECOND:SECOND + 1], eidf[:, bass.ds(t, 1)],
                                    xin[a][:, TOKEN:TOKEN + 1], ALU.is_equal, ALU.add).then_inc(t_dst, 1)
                kk, a, ok = live(k, r, 2, T, UN)
                if ok:
                    lo_x(UN * kk + a, a)

            def lo_x(t, a):
                dve.wait_ge(t_xhi, t + 1)
                v.tensor_tensor(xlo[a % 2][:, :], p_xT[:, 0:P], xhi[a % 2][:, :].bitcast(F32), ALU.subtract).then_inc(t_xlo, 1)

            def add_y(g, j, b, ybuf):
                n = GB * g + b
                xa = xs[:, n, :] if isinstance(n, int) else xs[:, bass.ds(n, 1), :].squeeze(1)
                w = wt[:, j, n:n + 1] if isinstance(n, int) else wt[:, j, bass.ds(n, 1)]
                return v.scalar_tensor_tensor(xa, ybuf, w, xa, ALU.mult, ALU.add)

            def late(g, i):
                def ybuf(b, j):
                    return yb[:, :, K * b + j, :][:, bass.ds(g, 1), :].squeeze(1)
                if i < GB:
                    if i == 0:
                        for a in range(HG):
                            dve.wait_ge(s_yb[a], 16)
                    add_y(g, 0, i, ybuf(i, 0)).then_inc(s_f1, 1)
                    if i:
                        dve.wait_ge(s_f1, GB * g + i)
                        ins = add_y(g, 1, i - 1, ybuf(i - 1, 1))
                elif i == GB:
                    dve.wait_ge(s_f1, GB * g + GB)
                    add_y(g, 1, GB - 1, ybuf(GB - 1, 1)).then_inc(s_f2, 1)

            dve.wait_ge(s_bias, 32)
            expert = [dve.alloc_register(f"expert{a}") for a in range(UN)]
            load_expert(0, 0)
            lo_x(0, 0)
            lo_x(1, 1)
            tile_loop(dve, tile_step, late)

            for g in range(HG, NG):
                dve.wait_ge(s_yb[g - HG], 32)
                for b in range(GB):
                    add_y(g, 0, b, yb[:, g - HG, K * b, :]).then_inc(s_f1, 1)
                for b in range(GB):
                    dve.wait_ge(s_f1, GB * g + b + 1)
                    ins = add_y(g, 1, b, yb[:, g - HG, K * b + 1, :])
                ins.then_inc(s_f2, 1)

        @block.tensor
        def _(pe):
            mm, tr = nc.tensor.matmul, nc.tensor.transpose
            pe.wait_ge(s_par, 48)
            pe.wait_ge(s_id, 4)
            for c in range(3):
                tr(bank[1][:, c * P:(c + 1) * P], wa[:, :] if c == 0 else wc[:, (c - 1) * P:c * P],
                   ident[:, :]).then_inc(s_wT, 1)
            pe.wait_ge(s_wTc, 3)

            def transpose4(dst_p, src, s):
                for b in range(GB):
                    ins = tr(dst_p[:, b * P:(b + 1) * P], src[:, b, :], ident[:, :])
                ins.then_inc(s, 1)

            def step(k, r):
                k0, a0, ok0 = live(k, r, 0, NG, 2)
                k1, a1, ok1 = live(k, r, -1, NG, 2)
                k2, a2, ok2 = live(k, r, -2, NG, 2)
                g0, g1, g2 = 2 * k0 + a0, 2 * k1 + a1, 2 * k2 + a2
                if ok0:
                    pe.wait_ge(s_enc[a0], 16 * (k0 + 1))
                    transpose4(p_encT, enc[:, a0], q["Tenc"])
                    pe.wait_ge(q["xn"], g0 + 1)
                    transpose4(p_xnT, xn[:, a0], q["Txn"])
                    pe.wait_ge(q["encc"], g0 + 1)
                    mm(p_G[:, :], waT[:, :], encT[:, :, :].rearrange("p b l -> p (b l)"), start=True, stop=True).then_inc(q["G"], 1)
                    wait(pe, q["Vc"], g0)
                    for b in range(GB):
                        ins = mm(p_V[:, b * P:(b + 1) * P], encT[:, b, :], wcT[:, 0, :], start=True, stop=True)
                    ins.then_inc(q["V"], 1)
                if ok1:
                    pe.wait_ge(q["al"], g1 + 1)
                    transpose4(p_alT, al, q["Tal"])
                if ok0:
                    pe.wait_ge(q["xnc"], g0 + 1)
                    pe.wait_ge(q["Gc"], g0 + 1)
                    for b in range(GB):
                        ins = mm(p_S[:, b * P:(b + 1) * P], xnT[:, a0, b, :], Gs[:, b, :], start=True, stop=True)
                    ins.then_inc(q["S"], 1)
                if ok1:
                    pe.wait_ge(q["alc"], g1 + 1)
                    pe.wait_ge(q["Vc"], g1 + 1)
                    for b in range(GB):
                        o = p_O[:, b * P:(b + 1) * P]
                        mm(o, xnT[:, a1, b, :], wcT[:, 1, :], start=True, stop=False)
                        ins = mm(o, alT[:, b, :], Vs[:, a1, b, :], start=False, stop=True)
                    ins.then_inc(q["O"], 1)
                if ok2:
                    pe.wait_ge(q["xm"], g2 + 1)
                    transpose4(p_xmT, xm[:, a2], q["Txm"])
                    pe.wait_ge(q["xmc"], g2 + 1)
                    if isinstance(g2, int) and g2 == HG + 1:
                        pe.wait_ge(s_route, 1)
                    for b in range(GB):
                        ins = mm(p_log[:, b * E:(b + 1) * E], xmT[:, b, :], wg[:, :], start=True, stop=True)
                    ins.then_inc(q["gate"], 1)

            def rank(h):
                pe.wait_ge(s_cnt, h + 1)
                pe.wait_ge(q["logc"], (HG + 1, NG)[h])
                rk = p_rank.rearrange("p (n e) -> p n e", e=E)
                mm(rk, tri[:, :], cnt[:, :, :], start=True, stop=False)
                for n in range(1, HB):
                    mm(rk[:, n:HB, :], ones_b[:, :], cnt[:, 0:HB - n, :], start=False, stop=n == HB - 1)
                for n in range(HB):
                    ins = mm(p_cnt, ones_b[:, :], cnt[:, n, :], start=n == 0, stop=n == HB - 1)
                ins.then_inc(s_rank, 1)

            step(0, 0)
            step(0, 1)
            with pe.Fori(1, 3) as k:
                step(k, 0)
                step(k, 1)
            step(3, 0)
            rank(0)
            step(3, 1)
            step(4, 0)
            step(4, 1)
            rank(1)

            def x_transpose(t, kk, a):
                pe.wait_ge(s_xin[a], 16 * (kk + 1))
                wait(pe, t_xlo, t)
                tr(p_xT[:, 0:P], xin[a][:, 0:P], ident[:, :]).then_inc(t_xT, 1)

            expert = [pe.alloc_register(f"expert{a}") for a in range(UN)]

            def tile_step(k, r):
                kk, a, ok = live(k, r, 0, T, UN)
                if ok:
                    t = UN * kk + a
                    ev = pe.snap(expert[a], min_val=0, max_val=E - 1)
                    pe.wait_ge(t_xlo, t + 1)
                    h = p_H[a % 2][:, :]
                    mm(h, xhi[a % 2][:, :], wi_hi[:, bass.ds(ev * M, M)], start=True, stop=False)
                    mm(h, xlo[a % 2][:, :], wi_hi[:, bass.ds(ev * M, M)], start=False, stop=False)
                    mm(h, xhi[a % 2][:, :], wi_lo[:, bass.ds(ev * M, M)], start=False, stop=True).then_inc(t_up, 1)
                kk, a, ok = live(k, r, 1, T, UN)
                if ok:
                    pe.reg_load(expert[a], eidi[0:1, bass.ds(UN * kk + a, 1)])
                kk, a, ok = live(k, r, -1, T, UN)
                if ok:
                    t = UN * kk + a
                    pe.wait_ge(t_gelu, t + 1)
                    for c in range(MC):
                        ins = tr(p_hT[a % 2][:, c * P:(c + 1) * P], hid[a % 2][:, c * P:(c + 1) * P], ident[:, :])
                    ins.then_inc(t_hT, 1)
                kk, a, ok = live(k, r, 2, T, UN)
                if ok:
                    x_transpose(UN * kk + a, kk, a)
                kk, a, ok = live(k, r, -2, T, UN)
                if ok:
                    t = UN * kk + a
                    ev = pe.snap(expert[a], min_val=0, max_val=E - 1)
                    pe.wait_ge(t_hc, t + 1)
                    wait(pe, t_y, t - 1)
                    for c in range(MC):
                        ins = mm(p_Y[a % 2][:, 0:P], hT[a % 2][:, c * P:(c + 1) * P], wo[:, bass.ds(ev * M + c * P, P)],
                                 start=c == 0, stop=c == MC - 1)
                    ins.then_inc(t_down, 1)

            pe.wait_ge(s_wlo, E * M // WCH)
            pe.wait_ge(s_wo, 64)
            pe.wait_ge(q["Gc"], NG)
            pe.wait_ge(q["x1"], NG)
            pe.wait_ge(q["xmc"], NG)
            x_transpose(0, 0, 0)
            x_transpose(1, 0, 1)
            pe.reg_load(expert[0], eidi[0:1, 0:1])
            tile_loop(pe, tile_step)


def kernel(x, ctx_1024, condB_pt, _lenS2, L0_xcond_W_a, L0_xcond_W_c, L0_ffn_W_gate, L0_ffn_W_in, L0_ffn_b_in,
           L0_ffn_W_out, L0_ffn_b_out):
    import numpy as _np
    import concourse.bacc as _bacc
    from concourse import mybir as _mybir
    from concourse.bass_utils import run_bass_kernel_spmd as _run

    ins = dict(x=x, ctx=ctx_1024, pt=condB_pt, lens=_lenS2, w_a=L0_xcond_W_a, w_c=L0_xcond_W_c, w_gate=L0_ffn_W_gate,
               w_in=L0_ffn_W_in, b_in=L0_ffn_b_in, w_out=L0_ffn_W_out, b_out=L0_ffn_b_out)
    nc = _bacc.Bacc("TRN2", target_bir_lowering=False, num_devices=1)
    arrays, args = {}, []
    for name, a in ins.items():
        a = _np.ascontiguousarray(a)
        arrays[f"in_{name}"] = a
        args.append(nc.dram_tensor(f"in_{name}", a.shape, _mybir.dt.from_np(a.dtype), kind="ExternalInput").ap())
    o = nc.dram_tensor("out", (NB, P, P), F32, kind="ExternalOutput").ap()
    build(nc, *args, o)
    r = _run(nc, [arrays], core_ids=[0])
    return r.results[0]["out"]
```

```python
import numpy as np
import concourse.bass as bass
from concourse import mybir
from contextlib import ExitStack

F32 = mybir.dt.float32
BF16 = mybir.dt.bfloat16
I32 = mybir.dt.int32
U32 = mybir.dt.uint32
U8 = mybir.dt.uint8
ALU = mybir.AluOpType
ACT = mybir.ActivationFunctionType
AX = mybir.AxisListType.X

P = 128
NB = 32
GB = 4
NG = NB // GB
NH = 2
HB = NB // NH
HG = NG // NH
E = 8
K = 2
M = 512
MC = M // P
T = NB * K + E - 1
FIRST = -(-(HB * P * K - E * (P - 1)) // P)
T0 = HB * K + E
ROW = 132
TOKEN, SECOND = P, P + 1
NROWS = NB * P * K
SKIP = 65536.0
UN = 12
NX = 6
WPC = 4
FILLS = 3
AHEAD = 11
DB = 2
EPS = 1e-5
WINDOW = 16.0
DEV_POW = 128.0


def build(nc, x, ctx_in, pt, lens, w_a, w_c, w_gate, w_in, b_in, w_out, b_out, out):
    slots = nc.dram_tensor("slots", [T * P, ROW], F32, kind="Internal").ap()
    eout = nc.dram_tensor("eout", [NROWS, P], F32, kind="Internal").ap()
    mask_d = nc.dram_tensor("mask_d", [NB, P], U8, kind="Internal").ap()
    gauss_d = nc.dram_tensor("gauss_d", [NB, P], F32, kind="Internal").ap()
    with ExitStack() as es:
        def sb(name, shape, dt=F32):
            return es.enter_context(nc.sbuf_tensor(name, shape, dt))

        def sem(name):
            return es.enter_context(nc.semaphore(name))

        bank = [es.enter_context(nc.psum_tensor(f"bank{i}", [P, 512], F32)) for i in range(8)]
        p_encT = p_G = bank[0]
        p_xnT, p_V, p_log, p_S, p_alT, p_O, p_xmT = bank[1], bank[2], bank[3], bank[4], bank[5], bank[6], bank[7]
        p_rank, p_cnt = bank[3][:, P:P + HB * E], bank[3][:, P + HB * E:P + HB * E + E]
        p_binT = bank[7]
        p_H, p_xT, p_Y = [bank[0], bank[1]], [bank[7], bank[4]], [bank[6], bank[2]]

        ident = sb("ident", [P, P])
        tri = sb("tri", [P, P], BF16)
        ones_b = sb("ones_b", [P, P], BF16)
        neg = sb("neg", [P, 512])
        mhalf, epsc, mone = sb("mhalf", [P, GB]), sb("epsc", [P, GB]), sb("mone", [P, GB])
        revidx = sb("revidx", [P, E])
        caps = sb("caps", [P, 16])
        ones8 = sb("ones8", [P, E])
        tilei = sb("tilei", [P, T])
        filler = sb("filler", [P, ROW])
        wa, wc = sb("wa", [P, P]), sb("wc", [P, 2 * P])
        waT, wcT = sb("waT", [P, P]), sb("wcT", [P, 2, P])
        wg = sb("wg", [P, E])
        wi, wo = sb("wi", [P, E * M]), sb("wo", [P, E * M])
        bin_r, binT = sb("bin_r", [E * MC, P]), sb("binT", [P, E * MC])
        boutb = sb("boutb", [P, E * P])
        ptc, lenc, lenf = sb("ptc", [NB, 1]), sb("lenc", [NB, 1], I32), sb("lenf", [NB, 1])
        idx = sb("idx", [NB, P])
        w_lo, w_hi = sb("w_lo", [NB, 1]), sb("w_hi", [NB, 1])
        below, dist, dist2 = sb("below", [NB, P]), sb("dist", [NB, P]), sb("dist2", [NB, P])
        above = sb("above", [NB, P])
        mask, gauss = sb("mask", [NB, P], U8), sb("gauss", [NB, P])
        xs = sb("xs", [P, NB, P])
        enc = sb("enc", [P, 2, GB, P])
        mk, gs = sb("mk", [P, 2, GB, P], U8), sb("gs", [P, 2, GB, P])
        st1, mv1 = sb("st1", [P, 2, GB, 6]), sb("mv1", [P, 2, GB, 2])
        ve1, rs1 = sb("ve1", [P, 2, GB]), sb("rs1", [P, 2, GB])
        mr1, nb1 = sb("mr1", [P, 2, GB]), sb("nb1", [P, 2, GB])
        st2, mv2 = sb("st2", [P, 2, GB, 6]), sb("mv2", [P, 2, GB, 2])
        ve2, rs2 = sb("ve2", [P, 2, GB]), sb("rs2", [P, 2, GB])
        xn, xnT = sb("xn", [P, 2, GB, P]), sb("xnT", [P, 2, GB, P])
        encT, Gs, Vs = sb("encT", [P, GB, P]), sb("Gs", [P, GB, P]), sb("Vs", [P, 2, GB, P])
        nmax, ssum, rinv = sb("nmax", [P, 2, GB]), sb("ssum", [P, 2, GB]), sb("rinv", [P, 2, GB])
        ex, al, alT = sb("ex", [P, GB, P]), sb("al", [P, GB, P]), sb("alT", [P, GB, P])
        xm, xmT = sb("xm", [P, 2, GB, P]), sb("xmT", [P, GB, P])
        rows = sb("rows", [P, NB, ROW])
        logits = sb("logits", [P, NB, E])
        idle_v, idle_p, idle_a = sb("idle_v", [1, 4]), sb("idle_p", [1, 1]), sb("idle_a", [1, 1])
        r1, r2, r3 = (sb(n, [P, HB, E]) for n in ("r1", "r2", "r3"))
        oh1, oh2 = sb("oh1", [P, HB, E]), sb("oh2", [P, HB, E])
        cnt = sb("cnt", [P, HB, E], BF16)
        m1, m2, k1, k2 = (sb(n, [P, HB]) for n in ("m1", "m2", "k1", "k2"))
        md, me = (sb(n, [P, HB]) for n in ("md", "me"))
        wt = sb("wt", [P, K, NB])
        nexp, cover = sb("nexp", [P, E]), sb("cover", [P, E, 16])
        tiles_e, base = sb("tiles_e", [P, E]), sb("base", [P, E])
        left, carry, start, lim, jump = (sb(n, [P, E]) for n in ("left", "carry", "start", "lim", "jump"))
        gap, cumx = sb("gap", [P, E]), sb("cumx", [P, E])
        ends = sb("ends", [P, 3, E])
        pos, over = sb("pos", [P, HB, E]), sb("over", [P, HB, E])
        slotf, slot = sb("slotf", [P, K, HB]), sb("slot", [P, K, NB], U32)
        ecmp, eraw = sb("ecmp", [P, T - FIRST, 3 * E]), sb("eraw", [P, T])
        eidf, eidi = sb("eidf", [P, T]), sb("eidi", [P, T], I32)
        xin = [sb(f"xin{i}", [P, ROW]) for i in range(UN)]
        xT = [sb(f"xT{i}", [P, P]) for i in range(2)]
        wi_t = [sb(f"wi_t{i}", [P, M]) for i in range(3)]
        pre = [sb(f"pre{i}", [P, MC, P]) for i in range(2)]
        hid = [sb(f"hid{i}", [P, MC, P]) for i in range(3)]
        ys = [sb(f"ys{i}", [P, P]) for i in range(UN)]
        dst = [sb(f"dst{i}", [P, 1], U32) for i in range(UN)]
        part = xm
        yb = sb("yb", [P, HG, GB * K, P])

        s_par, s_wg, s_win, s_wst, s_wo = sem("s_par"), sem("s_wg"), sem("s_win"), sem("s_wst"), sem("s_wo")
        s_x = [sem(f"s_x{a}") for a in range(2)]
        s_enc = [sem(f"s_enc{a}") for a in range(2)]
        s_winb = [sem(f"s_winb{a}") for a in range(2)]
        s_wi, s_bin = sem("s_wi"), sem("s_bin")
        s_bout = sem("s_bout")
        s_fill = [sem(f"s_fill{h}") for h in range(NH)]
        s_scat = [sem(f"s_scat{h}") for h in range(NH)]
        s_xin = [sem(f"s_xin{a}") for a in range(UN)]
        s_yst = [sem(f"s_yst{a}") for a in range(UN)]
        s_yb = [sem(f"s_yb{a}") for a in range(HG)]
        s_y0 = sem("s_y0")
        s_out, s_out0 = sem("s_out"), sem("s_out0")
        s_cst, s_id, s_fil2 = sem("s_cst"), sem("s_id"), sem("s_fil2")
        s_w1, s_w2, s_w3, s_g = sem("s_w1"), sem("s_w2"), sem("s_w3"), sem("s_g")
        s_wT, s_wTc = sem("s_wT"), sem("s_wTc")
        s_bT, s_bTc = sem("s_bT"), sem("s_bTc")
        names = ("st1 mv1 ve1 rs1 mr1 nb1 xn st2 mv2 ve2 rs2 xm Tenc encc Txn xnc G Gc V Vc S msk nmx exp rinv al "
                 "Tal alc O tanh x1 Txm xmc gate logc").split()
        q = {n: sem("q_" + n) for n in names}
        s_cnt, s_rank, s_rkc, s_slot = sem("s_cnt"), sem("s_rank"), sem("s_rkc"), sem("s_slot")
        s_r, s_ra, s_rp, s_route = sem("s_r"), sem("s_ra"), sem("s_rp"), sem("s_route")
        t_xT, t_xc, t_wi, t_up, t_pre, t_gelu = (sem("t_" + n) for n in "xT xc wi up pre gelu".split())
        t_down, t_y, t_dst = (sem("t_" + n) for n in "down y dst".split())
        s_idle, s_rows = sem("s_idle"), sem("s_rows")
        s_f1, s_ft, s_sum, s_f2 = sem("s_f1"), sem("s_ft"), sem("s_sum"), sem("s_f2")

        ov = out.rearrange("n q h -> q n h")
        block = es.enter_context(nc.Block())

        def wait(eng, s, value):
            if not (isinstance(value, int) and value <= 0):
                eng.wait_ge(s, value)

        def apart(eng, cell=0):
            if eng is nc.vector:
                nc.vector.memset(idle_v[:, cell:cell + 1], 0.0)
            else:
                nc.gpsimd.tensor_tensor(idle_p[:, :], mhalf[0:1, 0:1], mhalf[0:1, 0:1], ALU.add).then_inc(s_idle, 1)

        def live(k, r, d, n, u):
            v = r + d
            kk, rr = k + v // u, v % u
            return kk, rr, (not isinstance(kk, int)) or 0 <= kk * u + rr < n

        turns = (T - 2 * UN - 1) // UN

        def tile_loop(eng, step, late=None):
            for u in range(2 * UN - 1):
                step(u // UN, u % UN)
            with eng.Fori(1, 1 + turns) as k:
                for r in range(UN - 1, 2 * UN - 1):
                    step(k + r // UN, r % UN)
            first = (1 + turns) * UN + UN - 1
            for u in range(first, T + 3):
                step(u // UN, u % UN)
                if late:
                    late(*divmod(u - first, GB))
            if late:
                for i in range(T + 3 - first, HB):
                    late(*divmod(i, GB))

        @block.sync
        def _(sp):
            def load_x(k, a):
                g = 2 * k + a
                wait(sp, s_x[a], 16 * k)
                sp.dma_start(xs[:, bass.ds(GB * g, GB), :],
                             x[bass.ds(GB * g, GB)].rearrange("b q h -> q b h")).then_inc(s_x[a], 16)

            def load_ctx(k, a):
                g = 2 * k + a
                wait(sp, q["Tenc"], g - 1)
                sp.dma_start(enc[:, a], ctx_in[bass.ds(GB * g, GB)].rearrange("b l h -> l b h")).then_inc(s_enc[a], 16)

            def load_window(k, a):
                g = 2 * k + a
                wait(sp, q["al"], g - 1)
                sp.dma_start(mk[:, a].rearrange("p b l -> p (b l)"),
                             mask_d[bass.ds(GB * g, GB), :].rearrange("b l -> (b l)").partition_broadcast(P)
                             ).then_inc(s_winb[a], 16)
                sp.dma_start(gs[:, a].rearrange("p b l -> p (b l)"),
                             gauss_d[bass.ds(GB * g, GB), :].rearrange("b l -> (b l)").partition_broadcast(P)
                             ).then_inc(s_winb[a], 16)

            def copy_rows(k, a):
                g = 2 * k + a
                sp.wait_ge(q["xm"], g + 1)
                sp.dma_start(rows[:, bass.ds(GB * g, GB), 0:P], xm[:, a]).then_inc(s_rows, 16)
                sp.wait_ge(s_rows, 16 * (g + 1))

            load_x(0, 0)
            load_ctx(0, 0)
            sp.dma_start(wa[:, :], w_a).then_inc(s_par, 16)
            sp.dma_start(wc[:, :], w_c).then_inc(s_par, 16)
            sp.dma_start(ptc[:, :], pt.rearrange("(b o) -> b o", o=1)).then_inc(s_win, 16)
            sp.dma_start(lenc[:, :], lens.rearrange("(b o) -> b o", o=1)).then_inc(s_win, 16)
            load_x(0, 1)
            load_ctx(0, 1)
            sp.dma_start(wg[:, :], w_gate).then_inc(s_wg, 16)
            sp.dma_start(bin_r[:, :], b_in.rearrange("e (c m) -> (e c) m", m=P)).then_inc(s_bin, 16)
            sp.wait_ge(s_g, 2)
            sp.dma_start(mask_d, mask[:, :]).then_inc(s_wst, 16)
            sp.dma_start(gauss_d, gauss[:, :]).then_inc(s_wst, 16)
            sp.wait_ge(s_wst, 32)
            load_window(0, 0)
            load_x(1, 0)
            load_window(0, 1)
            load_x(1, 1)
            load_ctx(1, 0)
            load_x(2, 0)
            load_ctx(1, 1)
            load_window(1, 0)

            def step(k, r):
                kk, a, ok = live(k, r, 2, NG, 2)
                if ok:
                    load_ctx(kk, a)
                kk, a, ok = live(k, r, 1, NG, 2)
                if ok:
                    load_window(kk, a)
                kk, a, ok = live(k, r, 3, NG, 2)
                if ok:
                    load_x(kk, a)
                kk, a, ok = live(k, r, -2, NG, 2)
                if ok:
                    copy_rows(kk, a)

            step(1, 0)
            with sp.Fori(1, 2) as k:
                step(k, 1)
                step(k + 1, 0)
            for st in range(5, NG + 2):
                step(st // 2, st % 2)

            def load_tile(k, a):
                t = UN * k + a
                wait(sp, t_xT, t - UN + 1)
                wait(sp, t_dst, t - UN + 1)
                sp.dma_start(xin[a][:, :], slots[bass.ds(t * P, P), :]).then_inc(s_xin[a], 16)

            sp.wait_ge(s_scat[0], 16 * K * HB)
            for t in range(FIRST):
                load_tile(t // UN, t % UN)
            sp.wait_ge(s_scat[1], 16 * K * HB)
            k0 = FIRST // UN + 1
            for t in range(FIRST, k0 * UN):
                load_tile(t // UN, t % UN)
            with sp.Fori(k0, T // UN) as k:
                for r in range(UN):
                    load_tile(k, r)

            ev = eout.rearrange("(p n) d -> p n d", p=P)

            def load_y(g, s):
                sp.dma_start(yb[:, g % HG], ev[:, GB * K * g:GB * K * (g + 1), :]).then_inc(s, 16)

            for a in range(UN):
                sp.wait_ge(s_yst[a], 16 * len(range(a, T0, UN)))
            for i, t in enumerate(range(T // UN * UN, T)):
                if i % 3 == 0:
                    wait(sp, s_y0, 16 * (i // 3))
                    load_y(i // 3, s_y0)
                load_tile(t // UN, t % UN)
            sp.wait_ge(s_sum, HG - 2)
            sp.dma_start(ov[:, 0:GB * (HG - 2), :], xs[:, 0:GB * (HG - 2), :]).then_inc(s_out0, 16)
            for a in range(UN):
                sp.wait_ge(s_yst[a], 16 * len(range(a, T, UN)))
            for g in range(HG, NG):
                sp.wait_ge(s_sum, g - HG + 1)
                load_y(g, s_yb[g - HG])
            sp.dma_start(ov[:, GB * (HG - 2):HB, :], xs[:, GB * (HG - 2):HB, :]).then_inc(s_out0, 16)
            for g in range(HG, NG):
                sp.wait_ge(s_f2, g - HG + 1)
                sp.wait_ge(s_sum, g + 1)
                sp.dma_start(ov[:, GB * g:GB * (g + 1), :], xs[:, GB * g:GB * (g + 1), :]).then_inc(s_out, 16)
            sp.wait_ge(s_out0, 32)
            sp.wait_ge(s_out, 16 * HG)

        @block.gpsimd
        def _(pool):
            g = nc.gpsimd
            g.iota(idx[:, :], [[1, P]], base=0, channel_multiplier=0, allow_small_or_imprecise_dtypes=True).then_inc(s_cst, 1)
            g.memset(mhalf[:, :], -0.5).then_inc(s_cst, 1)
            g.memset(epsc[:, :], EPS).then_inc(s_cst, 1)
            g.memset(mone[:, :], -1.0).then_inc(s_cst, 1)
            g.memset(ident[:, :], 0.0).then_inc(s_id, 1)
            g.memset(tri[:, :], 1.0).then_inc(s_id, 1)
            pool.wait_ge(s_id, 2)
            g.affine_select(out=ident[:, :], in_=ident[:, :], compare_op=ALU.not_equal, fill=1.0,
                            base=0, pattern=[[-1, P]], channel_multiplier=1).then_inc(s_id, 1)
            g.affine_select(out=tri[:, :], in_=tri[:, :], compare_op=ALU.is_gt, fill=0.0,
                            base=0, pattern=[[1, P]], channel_multiplier=-1).then_inc(s_id, 1)
            g.memset(neg[:, :], -1e9).then_inc(s_cst, 1)
            g.memset(ones_b[:, :], 1.0).then_inc(s_cst, 1)
            g.memset(ones8[:, :], 1.0).then_inc(s_cst, 1)
            g.iota(revidx[:, :], [[-1, E]], base=E, channel_multiplier=0, allow_small_or_imprecise_dtypes=True).then_inc(s_cst, 1)
            g.iota(caps[:, :], [[P, 16]], base=0, channel_multiplier=0, allow_small_or_imprecise_dtypes=True).then_inc(s_cst, 1)
            g.iota(tilei[:, :], [[1, T]], base=0, channel_multiplier=0, allow_small_or_imprecise_dtypes=True).then_inc(s_cst, 1)
            g.memset(filler[:, 0:P], 0.0).then_inc(s_fil2, 1)
            g.memset(filler[:, P:ROW], SKIP).then_inc(s_fil2, 1)
            g.iota(rows[:, :, TOKEN], [[K, NB]], base=0, channel_multiplier=K * NB,
                   allow_small_or_imprecise_dtypes=True).then_inc(s_cst, 1)
            g.memset(rows[:, :, SECOND + 1:ROW], 0.0).then_inc(s_cst, 1)

            def rstd(mv, ve, rs, a, s_mv, s_ve, s_rs, n):
                pool.wait_ge(s_mv, n)
                g.tensor_tensor(ve[:, a], mv[:, a, :, 1], epsc[:, :], ALU.add).then_inc(s_ve, 1)
                pool.wait_ge(s_ve, n)
                g.tensor_tensor(rs[:, a], ve[:, a], mhalf[:, :], ALU.pow).then_inc(s_rs, 1)

            def rstd1(kk, a):
                n = 2 * kk + a + 1
                rstd(mv1, ve1, rs1, a, q["mv1"], q["ve1"], q["rs1"], n)
                pool.wait_ge(q["rs1"], n)
                g.tensor_tensor(mr1[:, a], mv1[:, a, :, 0], rs1[:, a], ALU.mult).then_inc(q["mr1"], 1)
                pool.wait_ge(q["mr1"], n)
                g.tensor_tensor(nb1[:, a], mr1[:, a], mone[:, :], ALU.mult).then_inc(q["nb1"], 1)

            def step(k, r, first=None, then=None):
                kk, a, ok = live(k, r, 2, NG, 2)
                if ok:
                    rstd1(kk, a)
                if first:
                    first()
                kk, a, ok = live(k, r, -1, NG, 2)
                if ok:
                    rstd(mv2, ve2, rs2, a, q["mv2"], q["ve2"], q["rs2"], 2 * kk + a + 1)
                if then:
                    then()

            def scatter(h, n0, n1):
                for n in range(n0, n1):
                    for j in range(K):
                        g.indirect_dma_start(slots, bass.IndirectOffsetOnAxis(ap=slot[:, j, n:n + 1], axis=0),
                                             rows[:, n, :], None).then_inc(s_scat[h], 16)

            rstd1(0, 0)
            rstd1(0, 1)
            step(0, 0)
            step(0, 1)
            with pool.Fori(1, 3) as k:
                step(k, 0)
                step(k, 1)

            def first_rows():
                pool.wait_ge(s_fill[0], 16 * FILLS)
                pool.wait_ge(s_slot, 1)
                pool.wait_ge(s_rows, 16 * HG)
                scatter(0, 0, 2)

            step(3, 0, first_rows)
            step(3, 1, lambda: scatter(0, 2, 5))
            step(4, 0, lambda: scatter(0, 5, 8))
            scatter(0, 8, HB)
            pool.wait_ge(s_fill[1], 16 * FILLS)
            pool.wait_ge(s_slot, 2)
            pool.wait_ge(s_rows, 16 * NG)

            def store_y(k, a):
                t = UN * k + a
                pool.wait_ge(t_y, t + 1)
                pool.wait_ge(t_dst, t + 1)
                if not isinstance(t, int):
                    pool.wait_ge(s_idle, t - t0 + 1)
                    apart(nc.gpsimd)
                g.indirect_dma_start(eout, bass.IndirectOffsetOnAxis(ap=dst[a][:, :], axis=0), ys[a][:, :], None,
                                     bounds_check=NROWS - 1, oob_is_err=False).then_inc(s_yst[a], 16)

            t0 = 0
            for i in range(HB):
                scatter(1, HB + i, HB + i + 1)
                for _ in range(0 if i < AHEAD else 2):
                    store_y(t0 // UN, t0 % UN)
                    t0 += 1
            while t0 % UN:
                store_y(t0 // UN, t0 % UN)
                t0 += 1
            apart(nc.gpsimd)

            def add_parts(gr, b0, i):
                pool.wait_ge(s_f1, GB * (gr + 1) - b0)
                pool.wait_ge(s_ft, gr + 1)
                xg = xs[:, bass.ds(GB * gr + b0, GB - b0), :]
                g.tensor_tensor(xg, xg, part[:, i, b0:GB, :], ALU.add).then_inc(s_sum, 1)

            with pool.Fori(t0 // UN, T // UN) as k:
                for a in range(UN):
                    store_y(k, a)
            for a in range(T % UN):
                store_y(T // UN, a)
                if a % GB == 0 and a // GB < HG - 2:
                    add_parts(a // GB, 0, a // GB % 2)
            for gr in range(HG - 2, HG):
                add_parts(gr, 0, gr % 2)
            for gr in range(HG, NG):
                add_parts(gr, DB, gr % 2)

        @block.scalar
        def _(act):
            sc = nc.scalar
            def fill(h, i):
                lo, hi = (0, T0) if h == 0 else (T0, T)
                t0, t1 = lo + (hi - lo) * i // FILLS, lo + (hi - lo) * (i + 1) // FILLS
                act.dma_start(slots[t0 * P:t1 * P, :].rearrange("(p j) d -> p j d", p=P),
                              filler[:, :].unsqueeze(1).to_broadcast([P, t1 - t0, ROW])).then_inc(s_fill[h], 16)

            def load_wi(i):
                n = E // WPC
                act.dma_start(wi[:, bass.ds(i * n * M, n * M)].rearrange("p (e m) -> p e m", e=n),
                              w_in[bass.ds(i * n, n)].rearrange("e d m -> d e m")).then_inc(s_wi, 16)

            def load_wo(i):
                n = E // WPC
                act.dma_start(wo[:, i * n * M:(i + 1) * n * M].rearrange("p (ec d) -> p ec d", d=P),
                              w_out[i * n:(i + 1) * n].rearrange("e (c m) d -> m (e c) d", m=P)).then_inc(s_wo, 16)

            act.wait_ge(s_wT, 3)
            for c in range(3):
                sc.activation(waT[:, :] if c == 0 else wcT[:, c - 1, :], bank[1][:, c * P:(c + 1) * P],
                              ACT.Copy).then_inc(s_wTc, 1)
            act.wait_ge(s_w3, 1)
            sc.activation(gauss[:, :], dist2[:, :], ACT.Exp, scale=-1.0 / DEV_POW).then_inc(s_g, 1)

            def evac(dst_ap, src, s_in, s_done, n):
                act.wait_ge(s_in, n)
                sc.activation(dst_ap, src.rearrange("p (b c) -> p b c", b=GB), ACT.Copy).then_inc(s_done, 1)

            def norm1(kk, a, b0=0, b1=GB):
                g = 2 * kk + a
                if b0 == 0:
                    act.wait_ge(q["nb1"], g + 1)
                for b in range(b0, b1):
                    ins = sc.activation(xn[:, a, b, :], xs[:, bass.ds(GB * g + b, 1), :].squeeze(1), ACT.Identity,
                                        scale=rs1[:, a, b:b + 1], bias=nb1[:, a, b:b + 1])
                if b1 == GB:
                    ins.then_inc(q["xn"], 1)

            def step(k, r, tokens_last=False):
                k0, a0, ok0 = live(k, r, 0, NG, 2)
                k1, a1, ok1 = live(k, r, -1, NG, 2)
                k2, a2, ok2 = live(k, r, -2, NG, 2)
                kf, af, okf = live(k, r, 1, NG, 2)
                kn, an, okn = live(k, r, 2, NG, 2)
                g0, g1, g2, gf = 2 * k0 + a0, 2 * k1 + a1, 2 * k2 + a2, 2 * kf + af
                if ok1:
                    evac(alT[:, :, :], p_alT[:, :], q["Tal"], q["alc"], g1 + 1)
                if okf:
                    evac(encT[:, :, :], p_encT[:, :], q["Tenc"], q["encc"], gf + 1)
                if ok0:
                    act.wait_ge(q["nmx"], g0 + 1)
                    for b in range(GB):
                        ins = sc.activation(ex[:, b, :], p_S[:, b * P:(b + 1) * P], ACT.Exp, bias=nmax[:, a0, b:b + 1],
                                            accum_out=ssum[:, a0, b:b + 1])
                    ins.then_inc(q["exp"], 1)
                if ok1:
                    act.wait_ge(q["O"], g1 + 1)
                    sc.activation(p_O[:, :], p_O[:, :], ACT.Tanh).then_inc(q["tanh"], 1)
                if okf:
                    evac(xnT[:, af], p_xnT[:, :], q["Txn"], q["xnc"], gf + 1)
                if ok2 and not tokens_last:
                    evac(xmT[:, :, :], p_xmT[:, :], q["Txm"], q["xmc"], g2 + 1)
                if okf:
                    evac(Gs[:, :, :], p_G[:, :], q["G"], q["Gc"], gf + 1)
                if okn:
                    norm1(kn, an, 0, 1)
                if okf:
                    evac(Vs[:, af], p_V[:, :], q["V"], q["Vc"], gf + 1)
                if ok2 and tokens_last:
                    evac(xmT[:, :, :], p_xmT[:, :], q["Txm"], q["xmc"], g2 + 1)
                if okn:
                    norm1(kn, an, 1, 2)
                if ok2:
                    act.wait_ge(q["gate"], g2 + 1)
                    sc.activation(logits[:, bass.ds(GB * g2, GB), :],
                                  p_log[:, 0:GB * E].rearrange("p (b e) -> p b e", b=GB), ACT.Copy).then_inc(q["logc"], 1)
                if okn:
                    norm1(kn, an, 2, GB)

            def gate_exp(h):
                act.wait_ge(s_ra, h + 1)
                sc.activation(me[:, :], md[:, :], ACT.Exp).then_inc(s_rp, 1)

            evac(encT[:, :, :], p_encT[:, :], q["Tenc"], q["encc"], 1)
            norm1(0, 0)
            evac(Gs[:, :, :], p_G[:, :], q["G"], q["Gc"], 1)
            evac(xnT[:, 0], p_xnT[:, :], q["Txn"], q["xnc"], 1)
            norm1(0, 1)
            evac(Vs[:, 0], p_V[:, :], q["V"], q["Vc"], 1)
            step(0, 0)
            act.wait_ge(s_bT, 1)
            sc.activation(binT[:, :], p_binT[:, 0:E * MC], ACT.Copy).then_inc(s_bTc, 1)
            step(0, 1)
            act.wait_ge(s_fil2, 2)
            fill(0, 0)
            fill(0, 1)
            with act.Fori(1, 3) as k:
                step(k, 0)
                load_wi(2 * k - 2)
                step(k, 1)
                load_wi(2 * k - 1)
            fill(0, 2)
            load_wo(0)
            step(3, 0, tokens_last=True)
            gate_exp(0)
            for i in range(FILLS):
                fill(1, i)
            load_wo(1)
            step(3, 1)
            load_wo(2)
            load_wo(3)
            step(4, 0)
            act.dma_start(boutb[:, :], b_out.rearrange("e m -> (e m)").partition_broadcast(P)).then_inc(s_bout, 16)
            step(4, 1)
            gate_exp(1)
            act.wait_ge(s_rp, 2)
            sc.activation(idle_a[:, :], me[0:1, 0:1], ACT.Gelu)

            def copy_x(t, a):
                act.wait_ge(t_xT, t + 1)
                sc.activation(xT[a % 2][:, :], p_xT[a % 2][:, 0:P], ACT.Copy).then_inc(t_xc, 1)

            def tile_step(k, r):
                kk, a, ok = live(k, r, 2, T, UN)
                if ok:
                    copy_x(UN * kk + a, a)
                kk, a, ok = live(k, r, 0, T, UN)
                if ok:
                    t = UN * kk + a
                    act.wait_ge(t_pre, t + 1)
                    wait(act, t_down, t - 2)
                    sc.activation(hid[a % 3][:, :, :], pre[a % 2][:, :, :], ACT.Gelu).then_inc(t_gelu, 1)

            def scale_y(g, b, y, i):
                n = GB * g + b
                return sc.activation(part[:, i, b, :], y, ACT.Copy, scale=wt[:, 1, n:n + 1])

            def late(g, b):
                if b == 0:
                    act.wait_ge(s_y0, 16 * (g + 1))
                    wait(act, s_sum, g - 1)
                ins = scale_y(g, b, yb[:, g, K * b + 1, :], g % 2)
                if b == GB - 1:
                    ins.then_inc(s_ft, 1)

            copy_x(0, 0)
            copy_x(1, 1)
            tile_loop(act, tile_step, late)

            for g in range(HG, NG):
                act.wait_ge(s_yb[g - HG], 16)
                act.wait_ge(s_sum, g - 1)
                for b in range(DB, GB):
                    ins = scale_y(g, b, yb[:, g - HG, K * b + 1, :], g % 2)
                ins.then_inc(s_ft, 1)

        @block.vector
        def _(dve):
            v = nc.vector
            def window():
                dve.wait_ge(s_win, 32)
                dve.wait_ge(s_cst, 1)
                v.tensor_copy(lenf[:, :], lenc[:, :]).then_inc(s_w1, 1)
                v.tensor_scalar(w_lo[:, :], ptc[:, :], -WINDOW, 0.0, ALU.add, ALU.max).then_inc(s_w1, 1)
                v.tensor_scalar(dist[:, :], idx[:, :], ptc[:, :], None, ALU.subtract).then_inc(s_w1, 1)
                dve.wait_ge(s_w1, 3)
                v.tensor_scalar(w_hi[:, :], ptc[:, :], WINDOW, lenf[:, :], ALU.add, ALU.min).then_inc(s_w2, 1)
                v.tensor_tensor(dist2[:, :], dist[:, :], dist[:, :], ALU.mult).then_inc(s_w3, 1)
                v.tensor_scalar(below[:, :], idx[:, :], w_lo[:, :], None, ALU.is_lt).then_inc(s_w2, 1)
                dve.wait_ge(s_w2, 2)
                v.tensor_scalar(above[:, :], idx[:, :], w_hi[:, :], None, ALU.is_gt).then_inc(s_w2, 1)
                dve.wait_ge(s_w2, 3)
                v.tensor_tensor(mask[:, :], above[:, :], below[:, :], ALU.max).then_inc(s_g, 1)

            def stats(src, st, mv, a, s_st, s_mv, n):
                for b in range(GB):
                    ins = v.bn_stats(st[:, a, b, :], src(b))
                ins.then_inc(s_st, 1)
                dve.wait_ge(s_st, n)
                apart(nc.vector, 2 if st is st1 else 3)
                for b in range(GB):
                    ins = v.bn_aggr(mv[:, a, b, :], st[:, a, b, :])
                ins.then_inc(s_mv, 1)

            def normalise(dstf, src, mv, rs, a, s_rs, s_done, n):
                dve.wait_ge(s_rs, n)
                for b in range(GB):
                    ins = v.tensor_scalar(dstf(b), src(b), mv[:, a, b, 0:1], rs[:, a, b:b + 1], ALU.subtract, ALU.mult)
                ins.then_inc(s_done, 1)

            def xsrc(g):
                return lambda b: xs[:, bass.ds(GB * g + b, 1), :].squeeze(1) if not isinstance(g, int) else xs[:, GB * g + b, :]

            def stats1(kk, a):
                g = 2 * kk + a
                dve.wait_ge(s_x[a], 16 * (kk + 1))
                stats(xsrc(g), st1, mv1, a, q["st1"], q["mv1"], g + 1)

            def step(k, r, more=lambda i: None):
                k0, a0, ok0 = live(k, r, 0, NG, 2)
                k1, a1, ok1 = live(k, r, -1, NG, 2)
                k2, a2, ok2 = live(k, r, -2, NG, 2)
                kf, af, okf = live(k, r, 1, NG, 2)
                kn, an, okn = live(k, r, 2, NG, 2)
                g0, g1, g2, gf = 2 * k0 + a0, 2 * k1 + a1, 2 * k2 + a2, 2 * kf + af
                if ok0:
                    dve.wait_ge(q["S"], g0 + 1)
                    dve.wait_ge(s_winb[a0], 32 * (k0 + 1))
                    apart(nc.vector, 1)
                    sv = p_S[:, :].rearrange("p (b l) -> p b l", b=GB)
                    v.copy_predicated(sv, mk[:, a0], neg[:, :].rearrange("p (b l) -> p b l", b=GB)).then_inc(q["msk"], 1)
                    more(0)
                    dve.wait_ge(q["msk"], g0 + 1)
                    v.tensor_reduce(nmax[:, a0, :], sv, AX, ALU.max, negate=True).then_inc(q["nmx"], 1)
                more(1)
                if ok2:
                    if isinstance(g2, int):
                        wait(dve, s_rows, 16 * (g2 - 1))
                    normalise(lambda b: xm[:, a2, b, :], xsrc(g2), mv2, rs2, a2, q["rs2"], q["xm"], g2 + 1)
                if okn:
                    stats1(kn, an)
                more(2)
                if ok0:
                    dve.wait_ge(q["exp"], g0 + 1)
                    v.reciprocal(rinv[:, a0, :], ssum[:, a0, :]).then_inc(q["rinv"], 1)
                    more(3)
                    wait(dve, q["Tal"], g0)
                    dve.wait_ge(q["rinv"], g0 + 1)
                    for b in range(GB):
                        ins = v.scalar_tensor_tensor(al[:, b, :], ex[:, b, :], rinv[:, a0, b:b + 1], gs[:, a0, b, :],
                                                     ALU.mult, ALU.mult)
                    ins.then_inc(q["al"], 1)
                more(4)
                if ok1:
                    dve.wait_ge(q["tanh"], g1 + 1)
                    v.tensor_tensor(xs[:, bass.ds(GB * g1, GB), :], p_O[:, :].rearrange("p (b h) -> p b h", b=GB),
                                    xs[:, bass.ds(GB * g1, GB), :], ALU.add).then_inc(q["x1"], 1)
                    more(5)
                    dve.wait_ge(q["x1"], g1 + 1)
                    apart(nc.vector, 0)
                    stats(xsrc(g1), st2, mv2, a1, q["st2"], q["mv2"], g1 + 1)
                more(6)

            stats1(0, 0)
            window()
            stats1(0, 1)
            step(0, 0)
            step(0, 1)
            with dve.Fori(1, 3) as k:
                step(k, 0)
                step(k, 1)

            links = [0]

            def link(ins):
                links[0] += 1
                ins.then_inc(s_r, 1)
                dve.wait_ge(s_r, links[0])

            def linked():
                if links[0]:
                    dve.wait_ge(s_r, links[0])
                links[0] += 1

            def wide(ap):
                return ap.unsqueeze(2).to_broadcast([P, HB, E])

            def route(h, i):
                n = slice(HB * h, HB * (h + 1))
                lg = logits[:, n, :]
                rev = revidx[:, :].unsqueeze(1).to_broadcast([P, HB, E])
                src, m, kx, oh = (lg, m1, k1, oh1) if i < 6 else (r3[:, :, :], m2, k2, oh2)
                if i == 0:
                    dve.wait_ge(q["logc"], HG * (h + 1))
                    dve.wait_ge(s_cst, 12)
                linked()
                if i in (0, 6):
                    v.tensor_reduce(m[:, :], src, AX, ALU.max).then_inc(s_r, 1)
                elif i in (1, 7):
                    v.tensor_tensor(r1[:, :, :], src, wide(m[:, :]), ALU.is_equal).then_inc(s_r, 1)
                elif i in (2, 8):
                    v.tensor_tensor(r2[:, :, :], r1[:, :, :], rev, ALU.mult).then_inc(s_r, 1)
                elif i in (3, 9):
                    v.tensor_reduce(kx[:, :], r2[:, :, :], AX, ALU.max).then_inc(s_r, 1)
                elif i in (4, 10):
                    v.tensor_tensor(oh[:, :, :], r2[:, :, :], wide(kx[:, :]), ALU.is_equal).then_inc(s_r, 1)
                elif i == 5:
                    v.scalar_tensor_tensor(r3[:, :, :], oh1[:, :, :], -3e38, lg, ALU.mult, ALU.add).then_inc(s_r, 1)
                elif i == 11:
                    v.tensor_tensor(cnt[:, :, :], oh1[:, :, :], oh2[:, :, :], ALU.add).then_inc(s_cnt, 1)
                    v.tensor_tensor(md[:, :], m2[:, :], m1[:, :], ALU.subtract).then_inc(s_ra, 1)
                    v.tensor_scalar(rows[:, n, SECOND], k2[:, :], -1.0, float(E), ALU.mult, ALU.add).then_inc(s_r, 1)

            filled = ends[:, 0, E - 1:E]

            def over_experts(ap):
                return ap[:, :].unsqueeze(1).to_broadcast([P, HB, E])

            def place(h):
                n = slice(HB * h, HB * (h + 1))
                dve.wait_ge(s_rank, h + 1)
                count, rank = p_cnt, p_rank.rearrange("p (n e) -> p n e", e=E)
                cum = ends[:, 0, :] if h == 0 else cumx[:, :]
                if h == 0:
                    link(v.tensor_scalar(nexp[:, :], count, -float(P - 1), None, ALU.add))
                else:
                    link(v.scalar_tensor_tensor(nexp[:, :], count, -float(P), left[:, :], ALU.add, ALU.add))
                link(v.tensor_tensor(cover[:, :, :], nexp[:, :].unsqueeze(2).to_broadcast([P, E, 16]),
                                     caps[:, :].unsqueeze(1).to_broadcast([P, E, 16]), ALU.is_gt))
                link(v.tensor_reduce(tiles_e[:, :], cover[:, :, :], AX, ALU.add))
                link(v.tensor_tensor_scan(cum, ones8[:, :], tiles_e[:, :], 0.0, ALU.mult, ALU.add))
                if h == 0:
                    v.tensor_scalar(lim[:, :], tiles_e[:, :], float(P), None, ALU.mult)
                    v.tensor_scalar(carry[:, :], tilei[:, 0:E], filled, None, ALU.add)
                    link(v.tensor_tensor(base[:, :], cum, tiles_e[:, :], ALU.subtract))
                    v.tensor_scalar(start[:, :], base[:, :], float(P), None, ALU.mult)
                    v.tensor_tensor(left[:, :], count, lim[:, :], ALU.subtract)
                    v.tensor_scalar(ends[:, 1, :], carry[:, :], 1.0, None, ALU.add)
                    link(v.tensor_tensor(gap[:, :], carry[:, :], cum, ALU.subtract))
                else:
                    v.tensor_scalar(lim[:, :], left[:, :], -1.0, float(P), ALU.mult, ALU.add)
                    v.scalar_tensor_tensor(start[:, :], carry[:, :], float(P), left[:, :], ALU.mult, ALU.add)
                    v.tensor_scalar(ends[:, 2, :], cum, filled, float(E), ALU.add, ALU.add)
                    link(v.tensor_tensor(base[:, :], cum, tiles_e[:, :], ALU.subtract))
                    link(v.scalar_tensor_tensor(gap[:, :], base[:, :], -1.0, revidx[:, :], ALU.add, ALU.add))
                v.tensor_tensor(over[:, :, :], rank, over_experts(lim), ALU.is_ge)
                v.tensor_tensor(pos[:, :, :], rank, over_experts(start), ALU.add).then_inc(s_rkc, 1)
                link(v.tensor_scalar(jump[:, :], gap[:, :], float(P), None, ALU.mult))
                link(v.tensor_tensor(over[:, :, :], over[:, :, :], over_experts(jump), ALU.mult))
                link(v.tensor_tensor(pos[:, :, :], pos[:, :, :], over[:, :, :], ALU.add))
                v.tensor_tensor(r1[:, :, :], oh1[:, :, :], pos[:, :, :], ALU.mult)
                link(v.tensor_tensor(r2[:, :, :], oh2[:, :, :], pos[:, :, :], ALU.mult))
                v.tensor_reduce(slotf[:, 0, :], r1[:, :, :], AX, ALU.add)
                link(v.tensor_reduce(slotf[:, 1, :], r2[:, :, :], AX, ALU.add))
                v.tensor_copy(slot[:, :, n], slotf[:, :, :]).then_inc(s_slot, 1)

            def tile_experts(h):
                n = slice(HB * h, HB * (h + 1))
                tt, kinds = (slice(0, FIRST), 1) if h == 0 else (slice(FIRST, T), 3)
                nt = tt.stop - tt.start
                cmp = ecmp[:, 0:nt, 0:kinds * E]
                link(v.tensor_tensor(cmp, ends[:, 0:kinds, :].rearrange("p k e -> p (k e)").unsqueeze(1).to_broadcast(
                    [P, nt, kinds * E]), tilei[:, tt].unsqueeze(2).to_broadcast([P, nt, kinds * E]), ALU.is_le))
                link(v.tensor_reduce(eraw[:, tt], cmp, AX, ALU.add))
                for kind in range(1, kinds):
                    link(v.scalar_tensor_tensor(eraw[:, tt], ecmp[:, 0:nt, kind * E - 1], -float(E), eraw[:, tt],
                                                ALU.mult, ALU.add))
                link(v.tensor_scalar(eidf[:, tt], eraw[:, tt], float(E - 1), None, ALU.min))
                link(v.tensor_copy(eidi[:, tt], eidf[:, tt]))
                dve.wait_ge(s_rp, h + 1)
                link(v.tensor_scalar(md[:, :], me[:, :], 1.0, None, ALU.add))
                link(v.reciprocal(wt[:, 0, n], md[:, :]))
                v.tensor_tensor(wt[:, 1, n], me[:, :], wt[:, 0, n], ALU.mult).then_inc(s_route, 1)

            for i in range(12):
                route(0, i)
            step(3, 0, lambda i: place(0) if i == 1 else None)
            step(3, 1)
            step(4, 0, lambda i: tile_experts(0) if i == 4 else None)
            step(4, 1)
            for i in range(12):
                route(1, i)
            place(1)
            tile_experts(1)

            def load_expert(kk, a):
                dve.reg_load(expert[a % NX], eidi[0:1, bass.ds(UN * kk + a, 1)])

            def copy_wi(a):
                ev = dve.snap(expert[a % NX], min_val=0, max_val=E - 1)
                v.tensor_copy(wi_t[a % 3][:, :], wi[:, bass.ds(ev * M, M)]).then_inc(t_wi, 1)

            def tile_step(k, r):
                kk, a, ok = live(k, r, -3, T, UN)
                if ok:
                    t = UN * kk + a
                    ev = dve.snap(expert[a % NX], min_val=0, max_val=E - 1)
                    dve.wait_ge(t_down, t + 1)
                    v.tensor_tensor(ys[a][:, :], p_Y[a % 2][:, 0:P], boutb[:, bass.ds(ev * P, P)], ALU.add).then_inc(t_y, 1)
                kk, a, ok = live(k, r, 0, T, UN)
                if ok:
                    t = UN * kk + a
                    ev = dve.snap(expert[a % NX], min_val=0, max_val=E - 1)
                    dve.wait_ge(t_up, t + 1)
                    wait(dve, t_gelu, t - 1)
                    v.tensor_tensor(pre[a % 2][:, :, :], p_H[a % 2][:, :].rearrange("p (c t) -> p c t", c=MC),
                                    binT[:, bass.ds(ev * MC, MC)].unsqueeze(2).to_broadcast([P, MC, P]), ALU.add
                                    ).then_inc(t_pre, 1)
                kk, a, ok = live(k, r, 2, T, UN)
                if ok:
                    load_expert(kk, a)
                    copy_wi(a)
                kk, a, ok = live(k, r, 0, T, UN)
                if ok:
                    t = UN * kk + a
                    wait(dve, s_yst[a], 16 * kk)
                    v.tensor_scalar(dst[a][:, :], xin[a][:, SECOND:SECOND + 1], eidf[:, bass.ds(t, 1)],
                                    xin[a][:, TOKEN:TOKEN + 1], ALU.is_equal, ALU.add).then_inc(t_dst, 1)

            def add_y(g, j, b, ybuf):
                n = GB * g + b
                return v.scalar_tensor_tensor(xs[:, n, :], ybuf, wt[:, j, n:n + 1], xs[:, n, :], ALU.mult, ALU.add)

            def late(g, b):
                if b == 0:
                    dve.wait_ge(s_y0, 16 * (g + 1))
                add_y(g, 0, b, yb[:, g, K * b, :]).then_inc(s_f1, 1)

            dve.wait_ge(s_bout, 16)
            dve.wait_ge(s_bTc, 1)
            expert = [dve.alloc_register(f"expert{a}") for a in range(NX)]
            dve.wait_ge(s_wi, 16 * WPC)
            for a in range(2):
                load_expert(0, a)
                copy_wi(a)
            tile_loop(dve, tile_step, late)

            for g in range(HG, NG):
                dve.wait_ge(s_yb[g - HG], 16)
                for b in [*range(DB, GB), *range(DB)]:
                    add_y(g, 0, b, yb[:, g - HG, K * b, :]).then_inc(s_f1, 1)
                for b in range(DB):
                    dve.wait_ge(s_f1, GB * (g + 1) - DB + b + 1)
                    ins = add_y(g, 1, b, yb[:, g - HG, K * b + 1, :])
                ins.then_inc(s_f2, 1)

        @block.tensor
        def _(pe):
            mm, tr = nc.tensor.matmul, nc.tensor.transpose

            def warm_up(n):
                for _ in range(n):
                    tr(bank[3][:, 0:P], ident[:, :], ident[:, :])

            pe.wait_ge(s_id, 4)
            warm_up(14)
            pe.wait_ge(s_par, 32)
            for c in range(3):
                tr(bank[1][:, c * P:(c + 1) * P], wa[:, :] if c == 0 else wc[:, (c - 1) * P:c * P],
                   ident[:, :]).then_inc(s_wT, 1)
            pe.wait_ge(s_wTc, 3)
            pe.wait_ge(s_bin, 16)
            tr(p_binT[:, 0:E * MC], bin_r[:, :], ident[0:E * MC, 0:E * MC]).then_inc(s_bT, 1)

            def transpose4(dst_p, src, s):
                for b in range(GB):
                    ins = tr(dst_p[:, b * P:(b + 1) * P], src[:, b, :], ident[:, :])
                ins.then_inc(s, 1)

            def context(kk, a):
                pe.wait_ge(s_enc[a], 16 * (kk + 1))
                transpose4(p_encT, enc[:, a], q["Tenc"])

            def tokens(kk, a):
                pe.wait_ge(q["xn"], 2 * kk + a + 1)
                transpose4(p_xnT, xn[:, a], q["Txn"])

            def key_product(kk, a):
                g = 2 * kk + a
                pe.wait_ge(q["encc"], g + 1)
                mm(p_G[:, :], waT[:, :], encT[:, :, :].rearrange("p b l -> p (b l)"), start=True, stop=True).then_inc(q["G"], 1)

            def value_product(kk, a):
                g = 2 * kk + a
                wait(pe, q["Vc"], g)
                for b in range(GB):
                    ins = mm(p_V[:, b * P:(b + 1) * P], encT[:, b, :], wcT[:, 0, :], start=True, stop=True)
                ins.then_inc(q["V"], 1)

            def products(kk, a):
                key_product(kk, a)
                value_product(kk, a)

            def step(k, r, ranks_of=None):
                k0, a0, ok0 = live(k, r, 0, NG, 2)
                k1, a1, ok1 = live(k, r, -1, NG, 2)
                k2, a2, ok2 = live(k, r, -2, NG, 2)
                kf, af, okf = live(k, r, 1, NG, 2)
                g0, g1, g2, gf = 2 * k0 + a0, 2 * k1 + a1, 2 * k2 + a2, 2 * kf + af
                if ok0:
                    pe.wait_ge(q["xnc"], g0 + 1)
                    pe.wait_ge(q["Gc"], g0 + 1)
                    wait(pe, q["exp"], g0)
                    for b in range(GB):
                        ins = mm(p_S[:, b * P:(b + 1) * P], xnT[:, a0, b, :], Gs[:, b, :], start=True, stop=True)
                    ins.then_inc(q["S"], 1)
                if ok0 and isinstance(g0, int) and g0 == 0:
                    value_product(k0, a0)
                if ok1:
                    pe.wait_ge(q["al"], g1 + 1)
                    transpose4(p_alT, al, q["Tal"])
                if okf:
                    context(kf, af)
                if ranks_of is not None:
                    rank(ranks_of)
                if ok1:
                    pe.wait_ge(q["alc"], g1 + 1)
                    pe.wait_ge(q["Vc"], g1 + 1)
                    wait(pe, q["x1"], g1)
                    for b in range(GB):
                        o = p_O[:, b * P:(b + 1) * P]
                        mm(o, xnT[:, a1, b, :], wcT[:, 1, :], start=True, stop=False)
                        ins = mm(o, alT[:, b, :], Vs[:, a1, b, :], start=False, stop=True)
                    ins.then_inc(q["O"], 1)
                if okf:
                    tokens(kf, af)
                if okf and ranks_of is not None:
                    products(kf, af)
                if ok2:
                    pe.wait_ge(q["xm"], g2 + 1)
                    transpose4(p_xmT, xm[:, a2], q["Txm"])
                if okf and ranks_of is None:
                    products(kf, af)
                if ok2:
                    pe.wait_ge(q["xmc"], g2 + 1)
                    if ranks_of is not None:
                        pe.wait_ge(s_rkc, ranks_of + 1)
                    for b in range(GB):
                        ins = mm(p_log[:, b * E:(b + 1) * E], xmT[:, b, :], wg[:, :], start=True, stop=True)
                    ins.then_inc(q["gate"], 1)

            def rank(h):
                pe.wait_ge(s_cnt, h + 1)
                pe.wait_ge(q["logc"], HG * (h + 1))
                rk = p_rank.rearrange("p (n e) -> p n e", e=E)
                mm(rk, tri[:, :], cnt[:, :, :], start=True, stop=False)
                for n in range(1, HB):
                    mm(rk[:, n:HB, :], ones_b[:, :], cnt[:, 0:HB - n, :], start=False, stop=n == HB - 1)
                for n in range(HB):
                    ins = mm(p_cnt, ones_b[:, :], cnt[:, n, :], start=n == 0, stop=n == HB - 1)
                ins.then_inc(s_rank, 1)

            context(0, 0)
            pe.wait_ge(s_wg, 16)
            key_product(0, 0)
            tokens(0, 0)
            step(0, 0)
            step(0, 1)
            pe.wait_ge(s_bTc, 1)
            with pe.Fori(1, 3) as k:
                step(k, 0)
                step(k, 1)
            step(3, 0, ranks_of=0)
            step(3, 1)
            step(4, 0)
            step(4, 1)
            rank(1)

            pe.wait_ge(s_slot, 2)
            warm_up(32)

            def x_transpose(t, kk, a):
                pe.wait_ge(s_xin[a], 16 * (kk + 1))
                wait(pe, t_xc, t - 1)
                tr(p_xT[a % 2][:, 0:P], xin[a][:, 0:P], ident[:, :]).then_inc(t_xT, 1)

            expert = [pe.alloc_register(f"expert{a}") for a in range(NX)]

            def tile_step(k, r):
                kk, a, ok = live(k, r, 0, T, UN)
                if ok:
                    t = UN * kk + a
                    pe.wait_ge(t_xc, t + 1)
                    pe.wait_ge(t_wi, t + 1)
                    wait(pe, t_pre, t - 1)
                    for c in range(MC):
                        ins = mm(p_H[a % 2][:, c * P:(c + 1) * P], wi_t[a % 3][:, c * P:(c + 1) * P], xT[a % 2][:, :],
                                 start=True, stop=True)
                    ins.then_inc(t_up, 1)
                kk, a, ok = live(k, r, 1, T, UN)
                if ok:
                    pe.reg_load(expert[a % NX], eidi[0:1, bass.ds(UN * kk + a, 1)])
                kk, a, ok = live(k, r, 2, T, UN)
                if ok:
                    x_transpose(UN * kk + a, kk, a)
                kk, a, ok = live(k, r, -2, T, UN)
                if ok:
                    t = UN * kk + a
                    ev = pe.snap(expert[a % NX], min_val=0, max_val=E - 1)
                    pe.wait_ge(t_gelu, t + 1)
                    wait(pe, t_y, t - 1)
                    for c in range(MC):
                        ins = mm(p_Y[a % 2][:, 0:P], hid[a % 3][:, c, :], wo[:, bass.ds(ev * M + c * P, P)],
                                 start=c == 0, stop=c == MC - 1)
                    ins.then_inc(t_down, 1)

            pe.wait_ge(s_wi, 16 * WPC)
            pe.wait_ge(s_wo, 16 * WPC)
            pe.wait_ge(q["Gc"], NG)
            pe.wait_ge(q["x1"], NG)
            pe.wait_ge(q["xmc"], NG)
            x_transpose(0, 0, 0)
            warm_up(6)
            x_transpose(1, 0, 1)
            warm_up(6)
            pe.reg_load(expert[0], eidi[0:1, 0:1])
            tile_loop(pe, tile_step)


def kernel(x, ctx_1024, condB_pt, _lenS2, L0_xcond_W_a, L0_xcond_W_c, L0_ffn_W_gate, L0_ffn_W_in, L0_ffn_b_in,
           L0_ffn_W_out, L0_ffn_b_out):
    import numpy as _np
    import concourse.bacc as _bacc
    from concourse import mybir as _mybir
    from concourse.bass_utils import run_bass_kernel_spmd as _run

    ins = dict(x=x, ctx=ctx_1024, pt=condB_pt, lens=_lenS2, w_a=L0_xcond_W_a, w_c=L0_xcond_W_c, w_gate=L0_ffn_W_gate,
               w_in=L0_ffn_W_in, b_in=L0_ffn_b_in, w_out=L0_ffn_W_out, b_out=L0_ffn_b_out)
    nc = _bacc.Bacc("TRN2", target_bir_lowering=False, num_devices=1)
    arrays, args = {}, []
    for name, a in ins.items():
        a = _np.ascontiguousarray(a)
        arrays[f"in_{name}"] = a
        args.append(nc.dram_tensor(f"in_{name}", a.shape, _mybir.dt.from_np(a.dtype), kind="ExternalInput").ap())
    o = nc.dram_tensor("out", (NB, P, P), F32, kind="ExternalOutput").ap()
    build(nc, *args, o)
    r = _run(nc, [arrays], core_ids=[0])
    return r.results[0]["out"]
```
